# Optimizing a Trainium2 kernel written in Bass

```python
import numpy as np
import jax
import jax.numpy as jnp

def _softmax(x, axis=-1):
    return jax.nn.softmax(x, axis=axis)

def _gelu(x):
    return jax.nn.gelu(x, approximate=True)

def _silu(x):
    return jax.nn.silu(x)

def _sigmoid(x):
    return jax.nn.sigmoid(x)

def _layernorm(x, axis=-1, eps=1e-05):
    m = jnp.mean(x, axis=axis, keepdims=True)
    v = jnp.var(x, axis=axis, keepdims=True)
    return (x - m) / jnp.sqrt(v + eps)

def _scatter_add(tgt, idx, src, axis=0):
    return tgt.at[idx].add(src)

def _segment_sum(src, seg, n):
    return jax.ops.segment_sum(src, seg, n)
kernel_name = 'mk_flamingo_gated_d1_seqx_r4_e6a9f2'

def setup_inputs(seed: int=0):
    np.random.seed(seed)
    _w = jnp.asarray

    def _rec_inputs():
        import jax
        import jax.numpy as jnp
        _rk = jax.random.key(seed)
        x = -0.0005207 + 1.001 * jax.random.normal(jax.random.fold_in(_rk, 1), (4, 512, 256), jnp.float32)
        _lenS = 512 - jax.random.randint(jax.random.fold_in(_rk, 7), (4,), 0, max(1, 512 // 4) + 1, jnp.int32)
        _lenS2 = 1024 - jax.random.randint(jax.random.fold_in(_rk, 8), (4,), 0, max(1, 1024 // 4) + 1, jnp.int32)
        _ctx_1024P = jax.random.normal(jax.random.fold_in(_rk, 11), (4, 16, 256), jnp.float32)
        _ctx_1024c = jax.random.dirichlet(jax.random.fold_in(_rk, 511), 0.3 * jnp.ones((16,), jnp.float32), (4, 1024))
        _ctx_1024t = jnp.einsum('bsk,bkd->bsd', _ctx_1024c, _ctx_1024P)
        _ctx_1024t = _ctx_1024t * jax.lax.rsqrt(jnp.mean(jnp.square(_ctx_1024t)) + 1e-12) * 0.953939
        ctx_1024 = -1.52775e-05 + 0.999936 * (_ctx_1024t + 0.3 * jax.random.normal(jax.random.fold_in(_rk, 611), (4, 1024, 256), jnp.float32))
        _g = jax.random.normal(jax.random.fold_in(_rk, 9001), (2, 1), jnp.float32)
        _g = jnp.sign(_g) * jnp.maximum(jnp.abs(_g), 1.0) + (_g == 0) * 1.0
        g_xattn = _g[0]
        g_ffn = _g[1]
        return (x, ctx_1024, g_xattn, g_ffn)
    x, ctx_1024, g_xattn, g_ffn = _rec_inputs()

    def _L0_xattn_setup():
        import jax, jax.numpy as jnp
        import numpy as np
        DIM = 256
        HEADS = 16
        DHEAD = 64
        INNER = HEADS * DHEAD
        EPS = 1e-05

        def layer_norm(x, g, b):
            mu = jnp.mean(x, axis=-1, keepdims=True)
            var = jnp.mean(jnp.square(x - mu), axis=-1, keepdims=True)
            return (x - mu) * jax.lax.rsqrt(var + EPS) * g + b

        def apply_rope(x, cos, sin):
            d2 = x.shape[-1] // 2
            x1, x2 = (x[..., :d2], x[..., d2:])
            return jnp.concatenate([x1 * cos - x2 * sin, x2 * cos + x1 * sin], axis=-1)
        key = jax.random.key(seed)
        ks = jax.random.split(key, 10)
        B, N, S = (8, 64, 1024)
        latents = jax.random.normal(ks[0], (B, N, DIM), dtype=jnp.float32)
        context = jax.random.normal(ks[1], (B, S, DIM), dtype=jnp.float32)
        cos = jax.random.uniform(ks[2], (S, DHEAD // 2), dtype=jnp.float32)
        sin = jax.random.uniform(ks[3], (S, DHEAD // 2), dtype=jnp.float32)
        init = lambda k, shp, fan_in: jax.random.normal(k, shp, dtype=jnp.float32) / np.sqrt(fan_in)
        return {'latents': latents, 'context': context, 'cos': cos, 'sin': sin, 'ln_lat_g': jnp.ones((DIM,), jnp.float32), 'ln_lat_b': jnp.zeros((DIM,), jnp.float32), 'ln_ctx_g': jnp.ones((DIM,), jnp.float32), 'ln_ctx_b': jnp.zeros((DIM,), jnp.float32), 'Wq': init(ks[4], (DIM, INNER), DIM), 'Wkv': init(ks[5], (DIM, 2 * INNER), DIM), 'Wo': init(ks[6], (INNER, DIM), INNER), 'bo': jnp.zeros((DIM,), jnp.float32)}
    _L0_xattn_all = _L0_xattn_setup()
    _L0_xattn_in = {k: v for k, v in _L0_xattn_all.items() if k in ('cos', 'sin', 'ln_lat_g', 'ln_lat_b', 'ln_ctx_g', 'ln_ctx_b', 'Wq', 'Wkv', 'Wo', 'bo')}
    del _L0_xattn_all

    def _L0_ffn_setup():
        import jax, jax.numpy as jnp
        import numpy as np
        B, S, D, H, E, K = (4, 512, 256, 1024, 4, 2)
        key = jax.random.key(seed)
        ks = jax.random.split(key, 7)
        s1 = 1.0 / np.sqrt(D)
        s2 = 1.0 / np.sqrt(H)
        return {'x': jax.random.normal(ks[0], (B, S, D), jnp.float32), 'w1': jax.random.uniform(ks[1], (E, D, H), jnp.float32, -s1, s1), 'b1': jax.random.uniform(ks[2], (E, H), jnp.float32, -s1, s1), 'w2': jax.random.uniform(ks[3], (E, H, D), jnp.float32, -s2, s2), 'b2': jax.random.uniform(ks[4], (E, D), jnp.float32, -s2, s2), 'wr': jax.random.uniform(ks[5], (D, E), jnp.float32, -s1, s1), 'br': jax.random.uniform(ks[6], (E,), jnp.float32, -s1, s1)}
    _L0_ffn_all = _L0_ffn_setup()
    _L0_ffn_in = {k: v for k, v in _L0_ffn_all.items() if k in ('w1', 'b1', 'w2', 'b2', 'wr', 'br')}
    del _L0_ffn_all
    return {'x': x, 'ctx_1024': ctx_1024, 'g_xattn': g_xattn, 'g_ffn': g_ffn, 'L0_xattn_cos': _L0_xattn_in['cos'], 'L0_xattn_sin': _L0_xattn_in['sin'], 'L0_xattn_ln_lat_g': _L0_xattn_in['ln_lat_g'], 'L0_xattn_ln_lat_b': _L0_xattn_in['ln_lat_b'], 'L0_xattn_ln_ctx_g': _L0_xattn_in['ln_ctx_g'], 'L0_xattn_ln_ctx_b': _L0_xattn_in['ln_ctx_b'], 'L0_xattn_Wq': _L0_xattn_in['Wq'], 'L0_xattn_Wkv': _L0_xattn_in['Wkv'], 'L0_xattn_Wo': _L0_xattn_in['Wo'], 'L0_xattn_bo': _L0_xattn_in['bo'], 'L0_ffn_w1': _L0_ffn_in['w1'], 'L0_ffn_b1': _L0_ffn_in['b1'], 'L0_ffn_w2': _L0_ffn_in['w2'], 'L0_ffn_b2': _L0_ffn_in['b2'], 'L0_ffn_wr': _L0_ffn_in['wr'], 'L0_ffn_br': _L0_ffn_in['br']}

def reference(x, ctx_1024, g_xattn, g_ffn, L0_xattn_cos, L0_xattn_sin, L0_xattn_ln_lat_g, L0_xattn_ln_lat_b, L0_xattn_ln_ctx_g, L0_xattn_ln_ctx_b, L0_xattn_Wq, L0_xattn_Wkv, L0_xattn_Wo, L0_xattn_bo, L0_ffn_w1, L0_ffn_b1, L0_ffn_w2, L0_ffn_b2, L0_ffn_wr, L0_ffn_br):
    import jax
    import jax.numpy as jnp

    def _L0_xattn_ref(latents, context, cos, sin, ln_lat_g, ln_lat_b, ln_ctx_g, ln_ctx_b, Wq, Wkv, Wo, bo):
        import jax, jax.numpy as jnp
        import numpy as np
        DIM = 256
        HEADS = 16
        DHEAD = 64
        INNER = HEADS * DHEAD
        EPS = 1e-05

        def layer_norm(x, g, b):
            mu = jnp.mean(x, axis=-1, keepdims=True)
            var = jnp.mean(jnp.square(x - mu), axis=-1, keepdims=True)
            return (x - mu) * jax.lax.rsqrt(var + EPS) * g + b

        def apply_rope(x, cos, sin):
            d2 = x.shape[-1] // 2
            x1, x2 = (x[..., :d2], x[..., d2:])
            return jnp.concatenate([x1 * cos - x2 * sin, x2 * cos + x1 * sin], axis=-1)
        b, n, _ = latents.shape
        s = context.shape[1]
        lat = layer_norm(latents, ln_lat_g, ln_lat_b)
        ctx = layer_norm(context, ln_ctx_g, ln_ctx_b)
        q = (lat @ Wq).reshape(b, n, HEADS, DHEAD).transpose(0, 2, 1, 3)
        kv = ctx @ Wkv
        k, v = jnp.split(kv, 2, axis=-1)
        k = k.reshape(b, s, HEADS, DHEAD).transpose(0, 2, 1, 3)
        v = v.reshape(b, s, HEADS, DHEAD).transpose(0, 2, 1, 3)
        k = apply_rope(k, cos[None, None], sin[None, None])
        scale = DHEAD ** (-0.5)
        attn = jnp.einsum('bhnd,bhsd->bhns', q, k) * scale
        attn = jnp.clip(attn, -11.0, 11.0)
        attn = jax.nn.softmax(attn, axis=-1)
        out = jnp.einsum('bhns,bhsd->bhnd', attn, v)
        out = out.transpose(0, 2, 1, 3).reshape(b, n, INNER)
        return out @ Wo + bo

    def _L0_ffn_ref(x, w1, b1, w2, b2, wr, br):
        import jax, jax.numpy as jnp
        import numpy as np
        B, S, D, H, E, K = (4, 512, 256, 1024, 4, 2)
        Bx, Sx, Dx = x.shape
        xf = x.reshape(-1, Dx)
        logits = xf @ wr + br
        topk_vals, topk_idx = jax.lax.top_k(logits, K)
        gates = jax.nn.softmax(topk_vals, axis=-1)
        h = jax.nn.gelu(jnp.einsum('nd,edh->enh', xf, w1) + b1[:, None, :], approximate=False)
        y = jnp.einsum('enh,ehd->end', h, w2) + b2[:, None, :]
        c = jnp.einsum('eh,ehd->ed', jax.nn.gelu(b1, approximate=False), w2) + b2
        c_sum = c.sum(axis=0)
        yt = jnp.transpose(y, (1, 0, 2))
        y_sel = jnp.take_along_axis(yt, topk_idx[:, :, None], axis=1)
        c_sel = c[topk_idx]
        out = jnp.einsum('nk,nkd->nd', gates, y_sel - c_sel + c_sum[None, None, :])
        return out.reshape(Bx, Sx, Dx)
    x = x + jnp.tanh(g_xattn[0]) * _L0_xattn_ref(_layernorm(x, axis=-1), ctx_1024, L0_xattn_cos, L0_xattn_sin, L0_xattn_ln_lat_g, L0_xattn_ln_lat_b, L0_xattn_ln_ctx_g, L0_xattn_ln_ctx_b, L0_xattn_Wq, L0_xattn_Wkv, L0_xattn_Wo, L0_xattn_bo)
    x = x + jnp.tanh(g_ffn[0]) * _L0_ffn_ref(_layernorm(x, axis=-1), L0_ffn_w1, L0_ffn_b1, L0_ffn_w2, L0_ffn_b2, L0_ffn_wr, L0_ffn_br)
    return x

_drawn_inputs = setup_inputs


def setup_inputs(seed=0):
    import zlib

    import numpy as np

    out = dict(_drawn_inputs(seed))
    spreads = {'L0_xattn_ln_lat_g': (1.0, 0.6),
     'L0_xattn_ln_lat_b': (0.0, 0.678),
     'L0_xattn_ln_ctx_g': (1.0, 0.2),
     'L0_xattn_ln_ctx_b': (0.0, 0.1),
     'L0_xattn_bo': (0.0, 0.1)}
    factors = {'L0_xattn_cos': 5.664, 'L0_xattn_sin': 5.633, 'L0_ffn_b1': 3.072, 'L0_ffn_br': 2.882}
    for name, (base, spread) in spreads.items():
        noise = np.random.default_rng([zlib.crc32(name.encode()), seed]).standard_normal(out[name].shape)
        drawn = base * np.exp(spread * noise) if base else spread * noise
        out[name] = jnp.asarray(drawn.astype(out[name].dtype))
    for name, factor in factors.items():
        out[name] = (out[name] * factor).astype(out[name].dtype)
    return out
```

```python
from contextlib import ExitStack

import concourse.bass as bass
from concourse import mybir

ALU = mybir.AluOpType
ACT = mybir.ActivationFunctionType
F32 = mybir.dt.float32
F32R = mybir.dt.float32r

EPS = 1e-5
CLIP = 11.0
EXP_LOW, EXP_HIGH = 1.6701700790245659e-05, 59874.14171519782


def flamingo_kernel(nc, x, ctx_in, g_xattn, g_ffn, cos, sin, lat_g, lat_b, ctx_g, ctx_b, w_q, w_kv, w_o, b_o,
                    w_1, b_1, w_2, b_2, w_r, b_r, out):
    P = 128
    B, N, D = x.shape
    S = ctx_in.shape[1]
    INNER = w_q.shape[1]
    HALF = cos.shape[1]
    DH = 2 * HALF
    E, _, HID = w_1.shape
    KT = D // P
    UNITS = INNER // (4 * DH)
    UW = 4 * DH
    ST = S // P
    NT = N // P
    CH = 4
    STEPS = 2 * CH
    BS = UNITS * STEPS
    PAIRS = 2 * UNITS
    MT = HID // P
    assert (P, KT, ST, NT, STEPS, DH, N) == (128, 2, 8, 4, ST, 64, 512)

    with ExitStack() as stack:
        def sb(name, shape, dt=F32):
            return stack.enter_context(nc.sbuf_tensor(name, [P] + shape, dt))

        def ps(name, width):
            return stack.enter_context(nc.psum_tensor(name, [P, width], F32))

        def sem(name):
            return stack.enter_context(nc.semaphore(name))

        big = [sb(f"big{i}", [4 * KT * 1024], F32R) for i in range(2)]
        wkv = big[0][:].rearrange("p (l k n) -> p l k n", l=2, k=KT)
        kst = big[1][:].rearrange("p (u h s) -> p u h s", u=2, h=4)
        acts = sb("acts", [8 * 1024], F32R)
        ctx_t = acts[:, 0:4 * S].rearrange("p (l k s) -> p l k s", l=2, k=KT)
        lat_t = acts[:, 4 * S:4 * S + 4 * N].rearrange("p (l k n) -> p l k n", l=2, k=KT)
        o_sp = acts[:, 4 * S + 4 * N:].rearrange("p (l q n) -> p l q n", l=2, q=2)
        x_t = acts[:].rearrange("p (l k n) -> p l k n", l=2, k=KT)
        q_hid = sb("q_hid", [8 * N], F32R)
        q_sp = q_hid[:].rearrange("p (r h l n) -> p r h l n", r=2, h=2, l=2)
        hid_sp = q_hid[:].rearrange("p (r l n) -> p r l n", r=4, l=2)
        wq = sb("wq", [2, KT * 4, 2, DH], F32R)
        wo = sb("wo", [2, 2, D], F32R)
        k_sp = sb("k_sp", [4, 2, DH], F32R)
        gb_sp = sb("gb_sp", [2, E * MT], F32R)

        val = sb("val", [2, ST, UW])
        wraw = val[:].rearrange("p u t n -> p (u t n)")
        prob = sb("prob", [2, 2, 2 * N])
        pall = prob[:].rearrange("p a h n -> p (a h n)")
        wkv_raw = pall.rearrange("p (u k w n) -> p u k w n", u=4, k=KT, w=2)
        acc = sb("acc", [2, 2 * N])
        xacc = sb("xacc", [B * NT, D])
        k_raw = sb("k_raw", [UW])
        rot_c = sb("rot_c", [UW])
        rot_s = sb("rot_s", [UW])
        k_rot = rot_c
        rows = sb("rows", [4, D])
        lat_r = sb("lat_r", [NT, D])
        c_aff = sb("c_aff", [KT, P])
        l_aff = sb("l_aff", [KT, 2 * P])
        recip = sb("recip", [N])
        cosb = sb("cosb", [ST, 2, HALF])
        sinb = sb("sinb", [ST, 2, HALF])
        w_raw = sb("w_raw", [2, UW])
        wq_twice = w_raw[:].rearrange("p k (h c) -> p (k h) c", c=DH).unsqueeze(2).to_broadcast([P, KT * 4, 2, DH])
        ident = sb("ident", [P])
        ones = sb("ones", [DH])
        mhalf = sb("mhalf", [8])
        eps = sb("eps", [8])
        c_bn = sb("c_bn", [4, 6])
        c_mv = sb("c_mv", [4, 2])
        c_rs = sb("c_rs", [4, 2])
        l_bn = sb("l_bn", [NT, 6])
        l_mv = sb("l_mv", [NT, 2])
        l_rs = sb("l_rs", [4, NT])
        affine = sb("affine", [4, KT])
        gates2 = sb("gates2", [4])
        b1t = sb("b1t", [E * MT])
        gb = sb("gb", [E * MT])
        wrt = sb("wrt", [KT, E])
        brb = sb("brb", [E])
        tgate = gates2[:, 2:3]
        fgate = gates2[:, 3:4]
        f_logit = rot_c[:, 0:64].rearrange("p (t e) -> p t e", e=E)
        f_tmp = rot_c[:, 64:128].rearrange("p (t e) -> p t e", e=E)
        f_rank = rot_c[:, 128:192].rearrange("p (t e) -> p t e", e=E)
        f_gate = rot_c[:, 192:256].rearrange("p (t e) -> p t e", e=E)
        f_max = rot_s[:, 0:16]
        f_sum = rot_s[:, 16:32]
        f_inv = rot_s[:, 32:48]
        f_mv = rot_s[:, 64:96].rearrange("p (t c) -> p t c", c=2)
        f_rs = rot_s[:, 96:128].rearrange("p (a t) -> p a t", a=2)
        f_bn = rot_s[:, 128:224].rearrange("p (t c) -> p t c", c=6)
        bo_b = k_raw[:]
        csum = recip[:, 0:D]
        f_rows = lat_r[:]
        b2b = rows[:]
        xt_raw = pall[:, 0:KT * N].rearrange("p (k n) -> p k n", k=KT)
        hid = pall[:, KT * N:KT * N + 4 * N].rearrange("p (r n) -> p r n", r=4)

        sc = [ps("sc0", 2 * N), ps("sc1", 2 * N)]
        pv = ps("pv", N)
        kv = ps("kv", 2 * UW)
        tr = ps("tr", N)
        mi = ps("mi", N)
        hb = [sc[0][:, 0:N], sc[0][:, N:2 * N]]
        yb = [sc[1], None]

        ld_ctx = [sem(f"ld_ctx{i}") for i in range(4)]
        ld_x = [sem("ld_x0"), sem("ld_x1")]
        ld_w = [sem(f"ld_w{i}") for i in range(4)]
        ld_small = sem("ld_small")
        ld_wq = sem("ld_wq")
        ld_wo = sem("ld_wo")
        const = sem("const")
        wkv_h = sem("wkv_h")
        wkv_ready = sem("wkv_ready")
        tanh_ready = sem("tanh_ready")
        c_st = sem("c_st")
        c_ag = sem("c_ag")
        c_e1 = sem("c_e1")
        c_rstd = sem("c_rstd")
        c_norm = sem("c_norm")
        c_tr = sem("c_tr")
        c_affd = sem("c_affd")
        c_ready = sem("c_ready")
        l_st = sem("l_st")
        l_ag = sem("l_ag")
        l_ch = sem("l_ch")
        l_scale = sem("l_scale")
        l_norm = sem("l_norm")
        l_tr = sem("l_tr")
        l_affd = sem("l_affd")
        l_ready = sem("l_ready")
        wq_high = sem("wq_high")
        wq_ready = sem("wq_ready")
        wo_high = sem("wo_high")
        wo_ready = sem("wo_ready")
        kv_ready = sem("kv_ready")
        kraw_out = sem("kraw_out")
        kv_out = sem("kv_out")
        rot1 = sem("rot1")
        rot2 = sem("rot2")
        rot = sem("rot")
        k_high = sem("k_high")
        k_ready = sem("k_ready")
        k_tr = sem("k_tr")
        kst_ready = sem("kst_ready")
        q_mm = sem("q_mm")
        q_high = sem("q_high")
        q_ready = sem("q_ready")
        sc_ready = [sem("sc_ready0"), sem("sc_ready1")]
        exp_done = [sem("exp_done0"), sem("exp_done1")]
        clamped = [sem("clamped0"), sem("clamped1")]
        summed = [sem("summed0"), sem("summed1")]
        pv_done = sem("pv_done")
        den_ready = sem("den_ready")
        rec_done = sem("rec_done")
        o_norm = sem("o_norm")
        o_high = sem("o_high")
        o_ready = sem("o_ready")
        wo_mm = sem("wo_mm")
        wo_out = sem("wo_out")
        f_ld = sem("f_ld")
        f_ldw = [sem("f_ldw0"), sem("f_ldw1")]
        f_bo = sem("f_bo")
        f_stat = sem("f_stat")
        f_agg = sem("f_agg")
        f_eps = sem("f_eps")
        f_rstd = sem("f_rstd")
        f_norm = sem("f_norm")
        f_tr = sem("f_tr")
        f_raw = sem("f_raw")
        f_xh = sem("f_xh")
        f_xready = sem("f_xready")
        f_lmm = sem("f_lmm")
        f_chain = sem("f_chain")
        f_diff = sem("f_diff")
        f_exp = sem("f_exp")
        f_gates = sem("f_gates")
        gb_done = sem("gb_done")
        gbh = sem("gbh")
        gb_ready = sem("gb_ready")
        w_high = [sem("w_high0"), sem("w_high1")]
        w_ready = [sem("w_ready0"), sem("w_ready1")]
        h_mm = sem("h_mm")
        h_act = sem("h_act")
        h_high = sem("h_high")
        h_ready = sem("h_ready")
        y_mm = sem("y_mm")
        y_out = sem("y_out")
        cs_mm = sem("cs_mm")
        cs_chain = sem("cs_chain")
        fin = sem("fin")
        stored = sem("stored")

        def step_no(b, u, s):
            return b * BS + (u * STEPS + s)

        def tile_no(b, t):
            return b * ST + t

        def kv_no(b, u, t):
            return b * BS + (u * ST + t)

        def pair_no(b, p):
            return b * PAIRS + p

        QH = N // 2

        TURN = BS - ST - 5
        NORM, SCALE, LOAD = TURN - 1, TURN - 2, TURN - 4
        L_TURN = TURN + ST
        L_AGG, L_NORM = SCALE - NT - 1, SCALE

        def wait(eng, semaphore, count):
            if not (isinstance(count, int) and count <= 0):
                eng.wait_ge(semaphore, count)

        def attention(eng, before, step):
            before()
            for s in range(STEPS):
                step(0, 0, s, False)
            with eng.Fori(0, B - 1) as b:
                for u in range(1, UNITS + 1):
                    for s in range(STEPS):
                        step(b + u // UNITS, u % UNITS, s, False)
            for u in range(1, UNITS):
                for s in range(STEPS):
                    step(B - 1, u, s, True)

        SLOTS = ST + 3

        def is_first(b, u):
            return isinstance(b, int) and b == 0 and u == 0

        def next_unit(b, u):
            return (b, u + 1) if u + 1 < UNITS else (b + 1, 0)

        def next_pair(b, p):
            return (b, p + 1) if p + 1 < PAIRS else (b + 1, 0)

        block = stack.enter_context(nc.Block())

        @block.sync
        def _(sp):
            def bcast(v):
                return v.rearrange("(a n) -> a n", a=1).to_broadcast([P, v.shape[0]])

            def load_ctx(b, t):
                wait(sp, c_tr, tile_no(b, t) - 3)
                src = ctx_in[b] if isinstance(b, int) else ctx_in[bass.ds(b, 1)].rearrange("a s d -> (a s) d")
                sp.dma_start(rows[:, t % 4, :], src[t * P:(t + 1) * P, :]).then_inc(ld_ctx[t % 4], 16)

            def load_wq(b, u):
                if isinstance(b, int) and b * UNITS + u == 1:
                    sp.wait_ge(wq_ready, 1)
                wait(sp, wo_ready, b * UNITS + u - 1)
                sp.dma_start(w_raw[:], w_q[:, u * UW:(u + 1) * UW].rearrange("(k p) n -> p k n", p=P)).then_inc(ld_wq, 16)

            def load_wo(b, u, last):
                if last and u == UNITS - 1:
                    sp.wait_ge(wo_ready, b * UNITS + u)
                else:
                    sp.wait_ge(wq_ready, b * UNITS + u + 2)
                sp.dma_start(w_raw[:], w_o[u * UW:(u + 1) * UW, :].rearrange("(q p) n -> p q n", p=P)).then_inc(ld_wo, 16)

            def load_wkv(u):
                for k in range(KT):
                    sp.dma_start(wkv_raw[:, u, k], w_kv[k * P:(k + 1) * P, :].rearrange("p (w n) -> p w n", w=2)
                                 [:, :, u * UW:(u + 1) * UW]).then_inc(ld_w[u], 16)

            def before():
                for t in range(4):
                    load_ctx(0, t)
                    if t == 1:
                        load_wkv(0)
                load_wq(0, 0)
                sp.dma_start(cosb[:, :, 0, :], cos.rearrange("(t p) c -> p t c", p=P)).then_inc(ld_small, 16)
                sp.dma_start(sinb[:, :, 1, :], sin.rearrange("(t p) c -> p t c", p=P)).then_inc(ld_small, 16)
                for u in range(1, UNITS):
                    load_wkv(u)
                    load_ctx(0, 3 + u)
                for t in range(3 + UNITS, ST):
                    load_ctx(0, t)

            def step(b, u, s, last):
                if s == 0:
                    nb, nu = next_unit(b, u)
                    if not (last and u == UNITS - 1):
                        load_wq(nb, nu)
                if s == 4:
                    load_wo(b, u, last)
                i = u * STEPS + s
                if not last and 0 <= i - LOAD < ST:
                    load_ctx(b + 1, i - LOAD)

            attention(sp, before, step)

            sp.wait_ge(k_tr, B * BS)
            sp.dma_start(bo_b, bcast(b_o)).then_inc(f_ld, 16)
            sp.dma_start(b2b, b_2.rearrange("(a e) n -> a e n", a=1).to_broadcast([P, E, D])).then_inc(f_ld, 16)
            sp.wait_ge(pv_done, B * BS)
            for e in range(E):
                for half, (w, view) in enumerate(((w_1, w_1[e].rearrange("(k p) n -> p k n", p=P)),
                                                  (w_2, w_2[e].rearrange("(m p) n -> p m n", p=P)))):
                    if e:
                        sp.wait_ge(w_ready[half], e)
                    n = view.shape[1]
                    sp.dma_start(wraw[:, half * 2048:half * 2048 + 2048].rearrange("p (k n) -> p k n", k=n),
                                 view).then_inc(f_ldw[half], 16)
            for t in range(NT):
                sp.wait_ge(fin, t + 1)
                sp.dma_start(out[t].rearrange("(a p) d -> p a d", p=P), xacc[:, t * NT:(t + 1) * NT, :]).then_inc(stored, 16)
            sp.wait_ge(stored, 16 * NT)

        @block.gpsimd
        def _(pool):
            g = nc.gpsimd

            def ctx_scale(b, t):
                pool.wait_ge(c_ag, tile_no(b, t) + 1)
                g.tensor_tensor(c_rs[:, t % 4, 0:1], c_mv[:, t % 4, 1:2], eps[:, 0:1], ALU.add).then_inc(c_e1, 1)
                pool.wait_ge(c_e1, tile_no(b, t) + 1)
                g.tensor_tensor(c_rs[:, t % 4, 1:2], c_rs[:, t % 4, 0:1], mhalf[:, 0:1], ALU.pow).then_inc(c_rstd, 1)

            def lat_scale(b):
                pool.wait_ge(l_ag, b * NT + NT)
                v = l_mv[:, :, 1]
                e1, r, w, e2 = (l_rs[:, i, :] for i in range(4))
                n = [b * 6]

                def chain(ins):
                    n[0] = n[0] + 1
                    ins.then_inc(l_ch, 1)
                    pool.wait_ge(l_ch, n[0])

                chain(g.tensor_tensor(e1, v, eps[:, 0:NT], ALU.add))
                chain(g.tensor_tensor(r, e1, mhalf[:, 0:NT], ALU.pow))
                chain(g.tensor_tensor(w, r, r, ALU.mult))
                chain(g.tensor_tensor(w, w, v, ALU.mult))
                chain(g.tensor_tensor(w, w, eps[:, 0:NT], ALU.add))
                chain(g.tensor_tensor(e2, w, mhalf[:, 0:NT], ALU.pow))
                g.tensor_tensor(e1, e2, r, ALU.mult).then_inc(l_scale, 1)

            def wq_low(b, u):
                pool.wait_ge(wq_high, b * UNITS + u + 1)
                g.tensor_tensor(wq[:, 1], wq_twice, wq[:, 0].bitcast(F32), ALU.subtract).then_inc(wq_ready, 1)

            def wo_low(b, u):
                pool.wait_ge(wo_high, b * UNITS + u + 1)
                g.tensor_tensor(wo[:, 1], w_raw[:], wo[:, 0].bitcast(F32), ALU.subtract).then_inc(wo_ready, 1)

            def rotate(b, u, t):
                n = kv_no(b, u, t)
                kh = k_raw[:].rearrange("p (h a c) -> p h a c", h=4, a=2)
                pool.wait_ge(kraw_out, n + 1)
                g.tensor_tensor(rot_s[:].rearrange("p (h a c) -> p h a c", h=4, a=2), kh[:, :, ::-1, :],
                                sinb[:, t].unsqueeze(1).to_broadcast([P, 4, 2, HALF]), ALU.mult).then_inc(rot2, 1)
                pool.wait_ge(rot1, n + 1)
                pool.wait_ge(rot2, n + 1)
                g.tensor_tensor(k_rot[:], rot_c[:], rot_s[:], ALU.add).then_inc(rot, 1)
                pool.wait_ge(k_high, n + 1)
                g.tensor_tensor(k_sp[:, :, 1, :], k_rot[:].rearrange("p (h c) -> p h c", h=4),
                                k_sp[:, :, 0, :].bitcast(F32), ALU.subtract).then_inc(k_ready, 1)

            def before():
                g.memset(ident[:], 0.0).then_inc(const, 1)
                g.memset(mhalf[:], -0.5).then_inc(const, 1)
                g.memset(eps[:], EPS).then_inc(const, 1)
                g.memset(ones[:], 1.0).then_inc(const, 1)
                pool.wait_ge(const, 4)
                g.affine_select(out=ident[:], in_=ident[:], compare_op=ALU.not_equal, fill=1.0, base=0,
                                pattern=[[-1, P]], channel_multiplier=1).then_inc(const, 1)
                for t in range(SLOTS):
                    if t < ST:
                        ctx_scale(0, t)
                    if t == 2:
                        lat_scale(0)
                    if t == 3:
                        wq_low(0, 0)
                        pool.wait_ge(const, 7)
                    if 0 <= t - 3 < ST:
                        rotate(0, 0, t - 3)

            def step(b, u, s, last):
                i = u * STEPS + s
                make = not (last and u == UNITS - 1)
                if make:
                    rotate(*next_unit(b, u), s)
                    if s == 3:
                        wq_low(*next_unit(b, u))
                if s == 7:
                    wo_low(b, u)
                if not last and 0 <= i - SCALE < ST:
                    ctx_scale(b + 1, i - SCALE)
                if not last and i == L_NORM - 1:
                    lat_scale(b + 1)

            attention(pool, before, step)

            for t in range(B):
                pool.wait_ge(f_agg, NT * (t + 1))
                sl = slice(NT * t, NT * (t + 1))
                g.tensor_scalar(f_rs[:, 0, sl], f_mv[:, sl, 1], EPS, None, ALU.add).then_inc(f_eps, 1)
                pool.wait_ge(f_eps, t + 1)
                g.tensor_tensor(f_rs[:, 1, sl], f_rs[:, 0, sl], mhalf[:, 0:NT], ALU.pow).then_inc(f_rstd, 1)
                pool.wait_ge(f_xh, t + 1)
                g.tensor_tensor(x_t[:, 1, :, t * N:(t + 1) * N], xt_raw, x_t[:, 0, :, t * N:(t + 1) * N].bitcast(F32),
                                ALU.subtract).then_inc(f_xready, 1)
            for e in range(E):
                for half in range(2):
                    pool.wait_ge(w_high[half], e + 1)
                    w = big[e % 2][:, half * 4096:(half + 1) * 4096].rearrange("p (l n) -> p l n", l=2)
                    g.tensor_tensor(w[:, 1, :], wraw[:, half * 2048:half * 2048 + 2048], w[:, 0, :].bitcast(F32),
                                    ALU.subtract).then_inc(w_ready[half], 1)

        @block.scalar
        def _(act):
            a = nc.scalar

            def bcast(v):
                return v.rearrange("(a n) -> a n", a=1).to_broadcast([P, v.shape[0]])

            def kst_out(b, u, t):
                act.wait_ge(k_tr, kv_no(b, u, t) + 1)
                a.activation(kst[:, u % 2, :, t * P:(t + 1) * P], tr[:].rearrange("p (h s) -> p h s", h=4),
                             ACT.Copy).then_inc(kst_ready, 1)

            def kv_evac(b, u, t):
                act.wait_ge(kv_ready, kv_no(b, u, t) + 1)
                wait(act, k_ready, kv_no(b, u, t))
                a.activation(k_raw[:], kv[:, 0:UW], ACT.Copy).then_inc(kraw_out, 1)
                a.activation(val[:, u % 2, t, :], kv[:, UW:2 * UW], ACT.Copy).then_inc(kv_out, 1)

            def ctx_affine(b, t, bank):
                act.wait_ge(c_tr, tile_no(b, t) + 1)
                wait(act, c_ready, tile_no(b, t))
                for dst in (ctx_t[:, 0, :, t * P:(t + 1) * P], c_aff):
                    for k in range(KT):
                        last = a.activation(dst[:, k, :], bank[:, k * P:(k + 1) * P], ACT.Identity,
                                            scale=affine[:, 2, k:k + 1], bias=affine[:, 3, k:k + 1])
                last.then_inc(c_affd, 1)

            def lat_affine(b, hf, bank):
                act.wait_ge(l_tr, b * 2 + hf + 1)
                wait(act, l_ready, b * 2 + hf)
                for dst in (lat_t[:, 0, :, hf * QH:(hf + 1) * QH], l_aff):
                    for k in range(KT):
                        last = a.activation(dst[:, k, :], bank[:, k * QH:(k + 1) * QH], ACT.Identity,
                                            scale=affine[:, 0, k:k + 1], bias=affine[:, 1, k:k + 1])
                last.then_inc(l_affd, 1)

            def k_round(b, u, t):
                wait(act, k_tr, kv_no(b, u, t))
                act.wait_ge(rot, kv_no(b, u, t) + 1)
                a.activation(k_sp[:, :, 0, :], k_rot[:].rearrange("p (h c) -> p h c", h=4), ACT.Copy).then_inc(k_high, 1)

            def o_round(b, p):
                act.wait_ge(o_norm, pair_no(b, p) + 1)
                a.activation(o_sp[:, 0, p % 2, :], recip[:], ACT.Copy).then_inc(o_high, 1)

            def wkv_round(u):
                act.wait_ge(ld_w[u], 16 * KT)
                for w in range(2):
                    last = a.activation(wkv[:, 0, :, w * INNER + u * UW:w * INNER + (u + 1) * UW], wkv_raw[:, u, :, w, :],
                                        ACT.Copy)
                last.then_inc(wkv_h, 1)

            def wq_round(b, u):
                act.wait_ge(ld_wq, (b * UNITS + u + 1) * 16)
                a.activation(wq[:, 0], wq_twice, ACT.Copy).then_inc(wq_high, 1)

            def wo_round(b, u):
                act.wait_ge(ld_wo, (b * UNITS + u + 1) * 16)
                a.activation(wo[:, 0], w_raw[:], ACT.Copy).then_inc(wo_high, 1)

            def q_round(b, p, h):
                act.wait_ge(q_mm, pair_no(b, p) * 2 + h + 1)
                a.activation(q_sp[:, p % 2, h, 0, :], mi[:], ACT.Copy).then_inc(q_high, 1)

            def exps(b, u, s, h):
                act.wait_ge(sc_ready[h], step_no(b, u, s) + 1)
                c, q = s % CH, pair_no(b, u * 2 + s // CH)
                wait(act, summed[h], q * 4 + (-2, -1, 1, 1)[c])
                a.activation(prob[:, s % 2, h, :], sc[h][:], ACT.Exp, scale=DH ** -0.5).then_inc(exp_done[h], 1)

            def before():
                act.dma_start(xacc[:, 0:NT, :], x[0].rearrange("(a p) d -> p a d", p=P)).then_inc(ld_x[0], 16)
                for i, v in enumerate((lat_g, lat_b, ctx_g, ctx_b)):
                    with nc.allow_non_contiguous_dma(reason="four small vectors"):
                        act.dma_start(affine[:, i, :], v.rearrange("(k p) -> p k", p=P)).then_inc(ld_small, 16)
                act.dma_start(gates2[:, 0:1], bcast(g_xattn)).then_inc(ld_small, 16)
                act.dma_start(gates2[:, 1:2], bcast(g_ffn)).then_inc(ld_small, 16)
                for t in range(1, B):
                    act.dma_start(xacc[:, t * NT:(t + 1) * NT, :], x[t].rearrange("(a p) d -> p a d", p=P)).then_inc(ld_x[1], 16)
                act.wait_ge(ld_small, 16 * 8)
                a.activation(gates2[:, 2:4], gates2[:, 0:2], ACT.Tanh).then_inc(tanh_ready, 1)
                for t in range(SLOTS):
                    if 0 <= t - 1 < UNITS:
                        wkv_round(t - 1)
                    if t == 2:
                        wq_round(0, 0)
                    if 0 <= t - 3 < ST:
                        kv_evac(0, 0, t - 3)
                    if 0 <= t - 4 < ST - 1:
                        kst_out(0, 0, t - 4)
                    if 0 <= t - 1 < ST:
                        ctx_affine(0, t - 1, sc[0][:, ((t - 1) % 2) * N:((t - 1) % 2 + 1) * N])
                    if t == 4:
                        for hf in range(2):
                            lat_affine(0, hf, sc[1][:, hf * N:(hf + 1) * N])
                    if 0 <= t - 6 < 2:
                        q_round(0, 0, t - 6)
                    if 0 <= t - 3 < ST:
                        k_round(0, 0, t - 3)

            def step(b, u, s, last):
                i = u * STEPS + s
                p, c = u * 2 + s // CH, s % CH
                make = not (last and u == UNITS - 1)
                exps(b, u, s, 0)
                exps(b, u, s, 1)
                if make:
                    kv_evac(*next_unit(b, u), s)
                if s == 0:
                    kst_out(b, u, ST - 1)
                elif make:
                    kst_out(*next_unit(b, u), s - 1)
                if c == 1 and not (is_first(b, u) and s == 1):
                    o_round(*((b, p - 1) if p else (b - 1, PAIRS - 1)))
                if s == 3 and make:
                    wq_round(*next_unit(b, u))
                if s == 7:
                    wo_round(b, u)
                if make:
                    k_round(*next_unit(b, u), s)
                if not last and 0 <= i - TURN < ST:
                    ctx_affine(b + 1, i - TURN, tr)
                if not last and 0 <= i - L_TURN < 2:
                    lat_affine(b + 1, i - L_TURN, tr)
                if c in (1, 2) and not (last and p == PAIRS - 1):
                    q_round(*next_pair(b, p), c - 1)

            attention(act, before, step)
            o_round(B - 1, PAIRS - 1)

            with nc.allow_non_contiguous_dma(reason="small"):
                act.dma_start(b1t[:], b_1.rearrange("e (m p) -> p (e m)", p=P)).then_inc(f_ld, 16)
                act.dma_start(wrt[:], w_r.rearrange("(k p) e -> p k e", p=P)).then_inc(f_ld, 16)
            act.dma_start(brb[:], bcast(b_r)).then_inc(f_ld, 16)
            for t in range(B):
                for k in range(KT):
                    act.wait_ge(f_tr, KT * t + k + 1)
                    if t and k == 0:
                        act.wait_ge(f_xready, t)
                        act.wait_ge(f_lmm, t)
                    a.activation(xt_raw[:, k, :], (tr, mi)[k][:], ACT.Copy).then_inc(f_raw, 1)
            act.wait_ge(f_diff, 1)
            a.activation(f_tmp, f_logit, ACT.Exp).then_inc(f_exp, 1)
            act.wait_ge(f_ld, 16 * 5)
            a.activation(gb[:], b1t[:], ACT.Gelu).then_inc(gb_done, 1)

            def gelu(n, e, m):
                act.wait_ge(h_mm, n + 1)
                if not (isinstance(n, int) and n < 4):
                    act.wait_ge(h_ready, n - 3)
                a.activation(hid[:, m % 4, :], hb[m % 2], ACT.Gelu, bias=b1t[:, e * MT + m:e * MT + m + 1]).then_inc(h_act, 1)

            for e in range(E):
                for m in range(MT):
                    gelu(e * B * MT + m, e, m)
                with act.Fori(1, B) as t:
                    for m in range(MT):
                        gelu(t * MT + (e * B * MT + m), e, m)

        @block.vector
        def _(dve):
            v = nc.vector

            def ctx_stats(b, t):
                dve.wait_ge(ld_ctx[t % 4], b * (16 * ST // 4) + 16 * (t // 4 + 1))
                v.bn_stats(c_bn[:, t % 4, :], rows[:, t % 4, :]).then_inc(c_st, 1)

            def ctx_aggregate(b, t):
                v.bn_aggr(c_mv[:, t % 4, :], c_bn[:, t % 4, :]).then_inc(c_ag, 1)

            def ctx_norm(b, t):
                dve.wait_ge(c_rstd, tile_no(b, t) + 1)
                v.tensor_scalar(rows[:, t % 4, :], rows[:, t % 4, :], c_mv[:, t % 4, 0:1], c_rs[:, t % 4, 1:2],
                                ALU.subtract, ALU.mult).then_inc(c_norm, 1)

            def ctx_low(b, t):
                dve.wait_ge(c_affd, tile_no(b, t) + 1)
                v.tensor_tensor(ctx_t[:, 1, :, t * P:(t + 1) * P], c_aff[:], ctx_t[:, 0, :, t * P:(t + 1) * P].bitcast(F32),
                                ALU.subtract).then_inc(c_ready, 1)

            def lat_stats(b, t):
                first = isinstance(b, int) and b == 0
                dve.wait_ge(ld_x[0 if first else 1], 16 if first else 16 * (B - 1))
                row = xacc[:, t, :] if isinstance(b, int) else xacc[:, bass.ds(b * NT + t, 1), :].rearrange("p a d -> p (a d)")
                v.bn_stats(l_bn[:, t, :], row).then_inc(l_st, 1)

            def lat_aggregate(b, t):
                v.bn_aggr(l_mv[:, t, :], l_bn[:, t, :]).then_inc(l_ag, 1)

            def lat_norm(b, t):
                dve.wait_ge(l_scale, b + 1)
                row = xacc[:, t, :] if isinstance(b, int) else xacc[:, bass.ds(b * NT + t, 1), :].rearrange("p a d -> p (a d)")
                v.tensor_scalar(lat_r[:, t, :], row, l_mv[:, t, 0:1], l_rs[:, 0, t:t + 1],
                                ALU.subtract, ALU.mult).then_inc(l_norm, 1)

            def lat_low(b, hf):
                dve.wait_ge(l_affd, b * 2 + hf + 1)
                sl = slice(hf * QH, (hf + 1) * QH)
                v.tensor_tensor(lat_t[:, 1, :, sl], l_aff[:], lat_t[:, 0, :, sl].bitcast(F32),
                                ALU.subtract).then_inc(l_ready, 1)

            def wkv_low(u):
                dve.wait_ge(wkv_h, u + 1)
                for w in range(2):
                    cols = slice(w * INNER + u * UW, w * INNER + (u + 1) * UW)
                    last = v.tensor_tensor(wkv[:, 1, :, cols], wkv_raw[:, u, :, w, :], wkv[:, 0, :, cols].bitcast(F32),
                                           ALU.subtract)
                last.then_inc(wkv_ready, 1)

            def rot_cos(b, u, t):
                dve.wait_ge(kraw_out, kv_no(b, u, t) + 1)
                v.tensor_tensor(rot_c[:].rearrange("p (h c) -> p h c", h=4), k_raw[:].rearrange("p (h c) -> p h c", h=4),
                                cosb[:, t].rearrange("p a c -> p (a c)").unsqueeze(1).to_broadcast([P, 4, DH]),
                                ALU.mult).then_inc(rot1, 1)

            def q_low(b, p, h):
                dve.wait_ge(q_high, pair_no(b, p) * 2 + h + 1)
                v.tensor_tensor(q_sp[:, p % 2, h, 1, :], mi[:], q_sp[:, p % 2, h, 0, :].bitcast(F32),
                                ALU.subtract).then_inc(q_ready, 1)

            def clamp(b, u, s, h):
                dve.wait_ge(exp_done[h], step_no(b, u, s) + 1)
                v.tensor_scalar(prob[:, s % 2, h, :], prob[:, s % 2, h, :], EXP_LOW, EXP_HIGH,
                                ALU.max, ALU.min).then_inc(clamped[h], 1)

            def sums(b, u, s, h):
                c, q = s % CH, pair_no(b, u * 2 + s // CH)
                if c == 0:
                    return
                dve.wait_ge(clamped[h], step_no(b, u, s) + 1)
                if c == 1:
                    wait(dve, den_ready, q)
                    v.tensor_tensor(acc[:, h, :], prob[:, 0, h, :], prob[:, 1, h, :], ALU.add).then_inc(summed[h], 1)
                else:
                    dve.wait_ge(summed[h], q * 4 + c - 1)
                    v.tensor_tensor(acc[:, h, :], acc[:, h, :], prob[:, s % 2, h, :], ALU.add).then_inc(summed[h], 1)

            def fold(b, p, h):
                dve.wait_ge(summed[h], pair_no(b, p) * 4 + 3)
                v.tensor_tensor(acc[:, h, 0:N], acc[:, h, 0:N], acc[:, h, N:2 * N], ALU.add).then_inc(summed[h], 1)

            def reciprocals(b, p):
                dve.wait_ge(den_ready, pair_no(b, p) + 1)
                v.reciprocal(recip[:], mi[:]).then_inc(rec_done, 1)

            def normalise(b, p):
                dve.wait_ge(pv_done, (pair_no(b, p) + 1) * CH)
                dve.wait_ge(rec_done, pair_no(b, p) + 1)
                v.tensor_tensor(recip[:], pv[:], recip[:], ALU.mult).then_inc(o_norm, 1)

            def o_low(b, p):
                dve.wait_ge(o_high, pair_no(b, p) + 1)
                v.tensor_tensor(o_sp[:, 1, p % 2, :], recip[:], o_sp[:, 0, p % 2, :].bitcast(F32),
                                ALU.subtract).then_inc(o_ready, 1)

            def residual(b, u, hf):
                dve.wait_ge(wo_mm, (b * UNITS + u) * 2 + hf + 1)
                if isinstance(b, int):
                    dst = xacc[:, b * NT + 2 * hf:b * NT + 2 * hf + 2, :]
                else:
                    dst = xacc[:, bass.ds(b * NT + 2 * hf, 2), :]
                v.scalar_tensor_tensor(dst, mi[:].rearrange("p (a d) -> p a d", a=2), tgate, dst,
                                       ALU.mult, ALU.add).then_inc(wo_out, 1)

            def before():
                for t in range(SLOTS):
                    if t < ST:
                        ctx_stats(0, t)
                        dve.wait_ge(c_st, t + 1)
                        ctx_aggregate(0, t)
                    if t == 1:
                        for i in range(NT):
                            lat_stats(0, i)
                            dve.wait_ge(l_st, i + 1)
                            lat_aggregate(0, i)
                    if 0 <= t - 1 < ST:
                        ctx_norm(0, t - 1)
                    if 0 <= t - 2 < UNITS:
                        wkv_low(t - 2)
                    if t == 2:
                        dve.wait_ge(ld_small, 16 * 8)
                        v.tensor_copy(cosb[:, :, 1, :], cosb[:, :, 0, :]).then_inc(const, 1)
                        v.tensor_scalar(sinb[:, :, 0, :], sinb[:, :, 1, :], -1.0, None, ALU.mult).then_inc(const, 1)
                        dve.wait_ge(const, 7)
                    if 0 <= t - 2 < ST:
                        ctx_low(0, t - 2)
                    if t == 3:
                        for i in range(NT):
                            lat_norm(0, i)
                    if t == 5:
                        lat_low(0, 0)
                        lat_low(0, 1)
                    if 0 <= t - 7 < 2:
                        q_low(0, 0, t - 7)
                    if 0 <= t - 3 < ST:
                        rot_cos(0, 0, t - 3)
                dve.wait_ge(tanh_ready, 1)

            def step(b, u, s, last):
                i = u * STEPS + s
                p = u * 2 + s // CH
                c = s % CH
                make = not (last and u == UNITS - 1)
                last_pair = (b, p - 1) if p else (b - 1, PAIRS - 1)
                has_last = not (is_first(b, u) and s < CH)
                if c >= 2 and not (last and p == PAIRS - 1):
                    q_low(*next_pair(b, p), c - 2)
                if c == 1 and has_last:
                    normalise(*last_pair)
                ct, lt = i - SCALE, i - L_AGG
                if not last and 0 <= ct < ST:
                    dve.wait_ge(c_st, tile_no(b + 1, ct) + 1)
                if not last and 0 <= lt < NT:
                    dve.wait_ge(l_st, (b + 1) * NT + lt + 1)
                clamp(b, u, s, 0)
                if not last and 0 <= ct < ST:
                    ctx_aggregate(b + 1, ct)
                if not last and 0 <= lt < NT:
                    lat_aggregate(b + 1, lt)
                clamp(b, u, s, 1)
                if make:
                    rot_cos(*next_unit(b, u), s)
                if not last and 0 <= i - TURN - 1 < ST:
                    ctx_low(b + 1, i - TURN - 1)
                if not last and 0 <= i - L_TURN - 1 < 2:
                    lat_low(b + 1, i - L_TURN - 1)
                sums(b, u, s, 0)
                if s in (2, 3) and not is_first(b, u):
                    residual(*((b, u - 1) if u else (b - 1, UNITS - 1)), s - 2)
                sums(b, u, s, 1)
                if c == CH - 1:
                    fold(b, p, 0)
                    fold(b, p, 1)
                if c == 0 and has_last:
                    reciprocals(*last_pair)
                if c == 1 and has_last:
                    o_low(*last_pair)
                if not last:
                    if 0 <= ct + 1 < ST:
                        ctx_stats(b + 1, ct + 1)
                    if 0 <= i - NORM < ST:
                        ctx_norm(b + 1, i - NORM)
                    if 0 <= lt + 1 < NT:
                        lat_stats(b + 1, lt + 1)
                    if 0 <= i - L_NORM < NT:
                        lat_norm(b + 1, i - L_NORM)

            attention(dve, before, step)
            reciprocals(B - 1, PAIRS - 1)
            normalise(B - 1, PAIRS - 1)
            o_low(B - 1, PAIRS - 1)
            residual(B - 1, UNITS - 1, 0)
            residual(B - 1, UNITS - 1, 1)

            w1v = [big[i][:, 0:4096].rearrange("p (l n) -> p l n", l=2) for i in range(2)]
            w2v = [big[i][:, 4096:8192].rearrange("p (l n) -> p l n", l=2) for i in range(2)]

            def split_high(e):
                for half, w in enumerate((w1v[e % 2], w2v[e % 2])):
                    dve.wait_ge(f_ldw[half], 16 * (e + 1))
                    v.tensor_copy(w[:, 0, :], wraw[:, half * 2048:half * 2048 + 2048]).then_inc(w_high[half], 1)

            dve.wait_ge(k_ready, B * BS)
            dve.wait_ge(f_ld, 16 * 5)
            for t in range(B):
                sl = slice(NT * t, NT * (t + 1))
                xs = xacc[:, sl, :]
                v.scalar_tensor_tensor(xs, bo_b.unsqueeze(1).to_broadcast([P, NT, D]), tgate, xs,
                                       ALU.mult, ALU.add).then_inc(f_bo, 1)
                dve.wait_ge(f_bo, t + 1)
                for i in range(NT):
                    v.bn_stats(f_bn[:, NT * t + i, :], xacc[:, NT * t + i, :]).then_inc(f_stat, 1)
                for i in range(NT):
                    dve.wait_ge(f_stat, NT * t + i + 1)
                    v.bn_aggr(f_mv[:, NT * t + i, :], f_bn[:, NT * t + i, :]).then_inc(f_agg, 1)
                wait(dve, f_tr, KT * t)
                dve.wait_ge(f_rstd, t + 1)
                for i in range(NT):
                    j = NT * t + i
                    v.tensor_scalar(f_rows[:, i, :], xacc[:, j, :], f_mv[:, j, 0:1], f_rs[:, 1, j:j + 1],
                                    ALU.subtract, ALU.mult).then_inc(f_norm, 1)
                dve.wait_ge(f_raw, KT * (t + 1))
                v.tensor_copy(x_t[:, 0, :, t * N:(t + 1) * N], xt_raw).then_inc(f_xh, 1)
                if t == 0:
                    split_high(0)

            n = [0]

            def chain(ins):
                n[0] += 1
                ins.then_inc(f_chain, 1)
                dve.wait_ge(f_chain, n[0])

            R = B * NT
            dve.wait_ge(f_lmm, B)
            chain(v.tensor_tensor(f_logit, kv[:, 0:R * E].rearrange("p (t e) -> p t e", e=E),
                                  brb[:].unsqueeze(1).to_broadcast([P, R, E]), ALU.add))
            chain(v.tensor_reduce(f_max, f_logit, mybir.AxisListType.X, ALU.max))
            for j in range(E):
                to = f_rank if j == 0 else f_gate
                for lo, hi, op in ((0, j + 1, ALU.is_gt), (j + 1, E, ALU.is_ge)):
                    if hi > lo:
                        chain(v.tensor_tensor(to[:, :, lo:hi], f_logit[:, :, j:j + 1].to_broadcast([P, R, hi - lo]),
                                              f_logit[:, :, lo:hi], op))
                if j:
                    chain(v.tensor_tensor(f_rank, f_rank, f_gate, ALU.add))
            v.tensor_tensor(f_logit, f_logit, f_max.unsqueeze(2).to_broadcast([P, R, E]), ALU.subtract).then_inc(f_diff, 1)
            dve.wait_ge(f_exp, 1)
            chain(v.scalar_tensor_tensor(f_gate, f_rank, 2.0, f_tmp, ALU.is_lt, ALU.mult))
            chain(v.tensor_reduce(f_sum, f_gate, mybir.AxisListType.X, ALU.add))
            chain(v.reciprocal(f_inv, f_sum))
            chain(v.scalar_tensor_tensor(f_gate, f_gate, fgate, f_inv.unsqueeze(2).to_broadcast([P, R, E]),
                                         ALU.mult, ALU.mult))
            chain(v.tensor_tensor(csum, b2b[:, 0, :], b2b[:, 1, :], ALU.add))
            for e in range(2, E):
                chain(v.tensor_tensor(csum, csum, b2b[:, e, :], ALU.add))
            dve.wait_ge(gb_done, 1)
            v.tensor_copy(gb_sp[:, 0, :], gb[:]).then_inc(gbh, 1)
            dve.wait_ge(gbh, 1)
            v.tensor_tensor(gb_sp[:, 1, :], gb[:], gb_sp[:, 0, :].bitcast(F32), ALU.subtract).then_inc(gb_ready, 1)

            def hidden(n, e, m):
                dve.wait_ge(h_act, n + 1)
                wait(dve, y_mm, n - 3)
                c = gb[:, e * MT + m:e * MT + m + 1]
                v.tensor_scalar(hid_sp[:, m % 4, 0, :], hid[:, m % 4, :], c, None, ALU.subtract).then_inc(h_high, 1)
                dve.wait_ge(h_high, n + 1)
                v.scalar_tensor_tensor(hid_sp[:, m % 4, 1, :], hid[:, m % 4, :], c, hid_sp[:, m % 4, 0, :].bitcast(F32),
                                       ALU.subtract, ALU.subtract).then_inc(h_ready, 1)

            def combine(e, t):
                dve.wait_ge(y_mm, (t + e * B + 1) * MT)
                for i in range(NT):
                    if isinstance(t, int):
                        row, gate = xacc[:, t * NT + i, :], f_gate[:, t * NT + i, e:e + 1]
                    else:
                        row = xacc[:, bass.ds(t * NT + i, 1), :].rearrange("p a d -> p (a d)")
                        gate = f_gate[:, bass.ds(t * NT + i, 1), e:e + 1].rearrange("p a d -> p (a d)")
                    v.scalar_tensor_tensor(row, yb[0][:, i * D:(i + 1) * D], gate, row,
                                           ALU.mult, ALU.add).then_inc(y_out, 1)
                if e == E - 1:
                    dve.wait_ge(y_out, (t + e * B + 1) * NT)
                    dst = xacc[:, t * NT:(t + 1) * NT, :] if isinstance(t, int) else xacc[:, bass.ds(t * NT, NT), :]
                    v.tensor_tensor(dst, dst, csum.unsqueeze(1).to_broadcast([P, NT, D]), ALU.add).then_inc(fin, 1)

            for e in range(E):
                for m in range(MT):
                    hidden(e * B * MT + m, e, m)
                if e == E - 1:
                    dve.wait_ge(cs_mm, E)
                    v.tensor_tensor(csum, pv[:, 0:D], csum, ALU.add).then_inc(cs_chain, 1)
                    dve.wait_ge(cs_chain, 1)
                    v.tensor_scalar(csum, csum, fgate, None, ALU.mult).then_inc(cs_chain, 1)
                    dve.wait_ge(cs_chain, 2)
                combine(e, 0)
                if e + 1 < E:
                    split_high(e + 1)
                with dve.Fori(1, B) as t:
                    for m in range(MT):
                        hidden((t + e * B) * MT + m, e, m)
                    combine(e, t)

        @block.tensor
        def _(pe):
            mm = nc.tensor.matmul

            def three(dst, lhs, rhs, start, stop, **kw):
                mm(dst, lhs(0), rhs(0), start=start, stop=False, **kw)
                mm(dst, lhs(0), rhs(1), start=False, stop=False, **kw)
                return mm(dst, lhs(1), rhs(0), start=False, stop=stop, **kw)

            def ctx_turn(b, t, bank):
                pe.wait_ge(c_norm, tile_no(b, t) + 1)
                for k in range(KT):
                    last = nc.tensor.transpose(bank[:, k * P:(k + 1) * P], rows[:, t % 4, k * P:(k + 1) * P], ident[:])
                last.then_inc(c_tr, 1)

            def lat_turn(b, hf, bank):
                pe.wait_ge(l_norm, b * NT + 2 * hf + 2)
                for i in range(2):
                    for k in range(KT):
                        last = nc.tensor.transpose(bank[:, k * QH + i * P:k * QH + (i + 1) * P],
                                                   lat_r[:, 2 * hf + i, k * P:(k + 1) * P], ident[:])
                last.then_inc(l_tr, 1)

            def q_make(b, p, h):
                pe.wait_ge(l_ready, 2 * b + 2)
                pe.wait_ge(wq_ready, b * UNITS + p // 2 + 1)
                c = (p % 2) * 2 + h
                for k in range(KT):
                    last = three(mi[:], lambda l: wq[:, l, k * 4 + c].rearrange("p a c -> p (a c)"),
                                 lambda l: lat_t[:, l, k, :], k == 0, k == KT - 1)
                last.then_inc(q_mm, 1)

            def kv_make(b, u, t):
                pe.wait_ge(c_ready, tile_no(b, t) + 1)
                wait(pe, kv_out, kv_no(b, u, t))
                for k in range(KT):
                    last = three(kv[:].rearrange("p (w n) -> p w n", w=2), lambda l: ctx_t[:, l, k, t * P:(t + 1) * P],
                                 lambda l: wkv[:, l, k, :].rearrange("p (w n) -> p w n", w=2)[:, :, u * UW:(u + 1) * UW],
                                 k == 0, k == KT - 1)
                last.then_inc(kv_ready, 1)

            def k_turn(b, u, t):
                pe.wait_ge(k_ready, kv_no(b, u, t) + 1)
                wait(pe, kst_ready, kv_no(b, u, t))
                for h in range(4):
                    last = nc.tensor.transpose(tr[:, h * P:(h + 1) * P],
                                               k_sp[:, h].rearrange("p l c -> p (l c)").bitcast(F32), ident[:])
                last.then_inc(k_tr, 1)

            def score(b, u, s, h):
                c, j, p = s % CH, s // CH, u * 2 + s // CH
                if h == 0:
                    pe.wait_ge(kst_ready, kv_no(b, u, 2 * c + 1) + 1)
                if c == 0:
                    pe.wait_ge(q_ready, pair_no(b, p) * 2 + h + 1)
                wait(pe, exp_done[h], step_no(b, u, s))
                for i in range(2):
                    t = 2 * c + i
                    for l in range(2):
                        last = mm(sc[h][:, i * N:(i + 1) * N], kst[:, u % 2, 2 * j + h, t * P:(t + 1) * P],
                                  q_sp[:, j, h, l, :], start=l == 0, stop=l == 1)
                last.then_inc(sc_ready[h], 1)

            def values(b, u, s):
                c, j, p = s % CH, s // CH, u * 2 + s // CH
                if c == 0:
                    wait(pe, o_norm, pair_no(b, p))
                for h in range(2):
                    pe.wait_ge(clamped[h], step_no(b, u, s) + 1)
                for i in range(2):
                    for h in range(2):
                        last = mm(pv[h * DH:(h + 1) * DH, :], val[:, u % 2, 2 * c + i, (2 * j + h) * DH:(2 * j + h + 1) * DH],
                                  prob[:, s % 2, h, i * N:(i + 1) * N], start=c == 0 and i == 0, stop=c == CH - 1 and i == 1)
                last.then_inc(pv_done, 1)

            def denominators(b, p):
                for h in range(2):
                    pe.wait_ge(summed[h], (pair_no(b, p) + 1) * 4)
                    last = mm(mi[h * DH:(h + 1) * DH, :], ones[:], acc[:, h, 0:N], start=True, stop=True)
                last.then_inc(den_ready, 1)

            def project(b, u, hf):
                pe.wait_ge(o_ready, pair_no(b, 2 * u + 1) + 1)
                pe.wait_ge(wo_ready, b * UNITS + u + 1)
                for i in range(2):
                    for j in range(2):
                        last = three(mi[:, i * D:(i + 1) * D], lambda l: o_sp[:, l, j, (2 * hf + i) * P:(2 * hf + i + 1) * P],
                                     lambda l: wo[:, l, j, :], j == 0, j == 1)
                last.then_inc(wo_mm, 1)

            def before():
                pe.wait_ge(const, 5)
                for t in range(SLOTS):
                    if 0 <= t - 3 < ST:
                        pe.wait_ge(wkv_ready, 1)
                        kv_make(0, 0, t - 3)
                    if 0 <= t - 4 < ST - 1:
                        k_turn(0, 0, t - 4)
                    if 0 <= t - 1 < ST:
                        wait(pe, c_affd, t - 2)
                        ctx_turn(0, t - 1, sc[0][:, ((t - 1) % 2) * N:((t - 1) % 2 + 1) * N])
                    if t == 4:
                        for hf in range(2):
                            lat_turn(0, hf, sc[1][:, hf * N:(hf + 1) * N])
                    if 0 <= t - 6 < 2:
                        wait(pe, q_ready, t - 6)
                        q_make(0, 0, t - 6)
                pe.wait_ge(wkv_ready, UNITS)

            def step(b, u, s, last):
                i = u * STEPS + s
                p, c = u * 2 + s // CH, s % CH
                make = not (last and u == UNITS - 1)
                nb, nu = next_unit(b, u)
                score(b, u, s, 0)
                score(b, u, s, 1)
                if make:
                    kv_make(nb, nu, s)
                if s == 0 or make:
                    if not last and 0 <= i - TURN - 1 < ST:
                        pe.wait_ge(c_affd, tile_no(b + 1, i - TURN - 1) + 1)
                    if not last and 0 <= i - L_TURN - 1 < 2:
                        pe.wait_ge(l_affd, 2 * (b + 1) + i - L_TURN)
                    k_turn(*((nb, nu, s - 1) if s else (b, u, ST - 1)))
                if c == 0 and not (is_first(b, u) and s == 0):
                    pe.wait_ge(q_ready, pair_no(b, p) * 2 + 2)
                    wait(pe, wo_out, (b * UNITS + u) * 2 - (2 if s == 0 else 0))
                    denominators(*((b, p - 1) if p else (b - 1, PAIRS - 1)))
                if s in (2, 3) and not is_first(b, u):
                    if not (last and p == PAIRS - 1):
                        pe.wait_ge(q_ready, pair_no(b, p + 1) * 2 + c - 1)
                    wait(pe, wo_out, (b * UNITS + u) * 2 + s - 4)
                    project(*((b, u - 1) if u else (b - 1, UNITS - 1)), s - 2)
                if not (is_first(b, u) and s == 0):
                    values(*((b, u, s - 1) if s else (b, u - 1, STEPS - 1) if u else (b - 1, UNITS - 1, STEPS - 1)))
                if c in (1, 2) and not (last and p == PAIRS - 1):
                    wait(pe, rec_done, pair_no(b, p))
                    if s == 2:
                        wait(pe, wo_out, (b * UNITS + u) * 2 - 1)
                    if c == 2:
                        pe.wait_ge(q_ready, pair_no(b, p + 1) * 2 + 1)
                    q_make(*next_pair(b, p), c - 1)
                if not last and TURN <= i < L_TURN + 2:
                    pe.wait_ge(kst_ready, kv_no(nb, nu, s - 1) + 1 if s else kv_no(b, u, ST - 1) + 1)
                    if i < L_TURN:
                        ctx_turn(b + 1, i - TURN, tr)
                    else:
                        lat_turn(b + 1, i - L_TURN, tr)

            attention(pe, before, step)
            values(B - 1, UNITS - 1, STEPS - 1)
            denominators(B - 1, PAIRS - 1)
            pe.wait_ge(rec_done, B * PAIRS)
            project(B - 1, UNITS - 1, 0)
            pe.wait_ge(wo_out, B * UNITS * 2 - 1)
            project(B - 1, UNITS - 1, 1)
            pe.wait_ge(wo_out, B * UNITS * 2)

            w1v = [big[i][:, 0:4096].rearrange("p (l k n) -> p l k n", l=2, k=KT) for i in range(2)]
            w2v = [big[i][:, 4096:8192].rearrange("p (l m n) -> p l m n", l=2, m=MT) for i in range(2)]
            for t in range(B):
                pe.wait_ge(f_norm, NT * (t + 1))
                for k in range(KT):
                    wait(pe, f_raw, KT * (t - 1) + k + 1)
                    for i in range(NT):
                        last = nc.tensor.transpose((tr, mi)[k][:, i * P:(i + 1) * P], f_rows[:, i, k * P:(k + 1) * P], ident[:])
                    last.then_inc(f_tr, 1)
                pe.wait_ge(f_raw, KT * (t + 1))
                pe.wait_ge(f_ld, 16 * 5)
                for i in range(NT):
                    for k in range(KT):
                        last = mm(kv[:, (t * NT + i) * E:(t * NT + i + 1) * E], xt_raw[:, k, i * P:(i + 1) * P], wrt[:, k, :],
                                  start=k == 0, stop=k == KT - 1)
                last.then_inc(f_lmm, 1)
            pe.wait_ge(f_xready, B)

            def hidden(n, e, t, m):
                wait(pe, h_act, n - 1)
                for k in range(KT):
                    x_at = x_t[:, :, k, t * N:(t + 1) * N] if isinstance(t, int) else x_t[:, :, k, bass.ds(t * N, N)]
                    last = three(hb[m % 2], lambda l: w1v[e % 2][:, l, k, m * P:(m + 1) * P], lambda l: x_at[:, l, :],
                                 k == 0, k == KT - 1)
                last.then_inc(h_mm, 1)

            def outputs(n, e, t, m):
                pe.wait_ge(h_ready, n + 1)
                if m == 0:
                    wait(pe, y_out, (t + e * B) * NT)
                for i in range(NT):
                    last = three(yb[0][:, i * D:(i + 1) * D], lambda l: hid_sp[:, m % 4, l, i * P:(i + 1) * P],
                                 lambda l: w2v[e % 2][:, l, m, :], m == 0 and i % 2 == 0, m == MT - 1 and i % 2 == 1,
                                 skip_group_check=True)
                last.then_inc(y_mm, 1)

            def block_of(e, t, more):
                for m in range(MT):
                    outputs((t + e * B) * MT + m, e, t, m)
                    if m + 2 < MT or more:
                        hidden((t + e * B) * MT + m + 2, e, t + (m + 2) // MT, (m + 2) % MT)

            for e in range(E):
                pe.wait_ge(w_ready[0], e + 1)
                hidden(e * B * MT, e, 0, 0)
                hidden(e * B * MT + 1, e, 0, 1)
                pe.wait_ge(w_ready[1], e + 1)
                if e == 0:
                    pe.wait_ge(gb_ready, 1)
                for m in range(MT):
                    last = three(pv[:, 0:D], lambda l: gb_sp[:, l, e * MT + m:e * MT + m + 1].to_broadcast([P, P]),
                                 lambda l: w2v[e % 2][:, l, m, :], e == 0 and m == 0, e == E - 1 and m == MT - 1)
                last.then_inc(cs_mm, 1)
                with pe.Fori(0, B - 1) as t:
                    block_of(e, t, True)
                block_of(e, B - 1, False)


INPUTS = ["x", "ctx_1024", "g_xattn", "g_ffn", "L0_xattn_cos", "L0_xattn_sin", "L0_xattn_ln_lat_g", "L0_xattn_ln_lat_b",
          "L0_xattn_ln_ctx_g", "L0_xattn_ln_ctx_b", "L0_xattn_Wq", "L0_xattn_Wkv", "L0_xattn_Wo", "L0_xattn_bo",
          "L0_ffn_w1", "L0_ffn_b1", "L0_ffn_w2", "L0_ffn_b2", "L0_ffn_wr", "L0_ffn_br"]


def kernel(**inputs):
    import numpy as np
    import concourse.bacc as bacc
    from concourse.bass_utils import run_bass_kernel_spmd

    nc = bacc.Bacc("TRN2", target_bir_lowering=False, num_devices=1)
    arrays, args = {}, []
    for name in INPUTS:
        value = np.ascontiguousarray(inputs[name])
        arrays[f"in_{name}"] = value
        args.append(nc.dram_tensor(f"in_{name}", value.shape, mybir.dt.from_np(value.dtype), kind="ExternalInput").ap())
    shape = inputs["x"].shape
    args.append(nc.dram_tensor("out", shape, F32, kind="ExternalOutput").ap())
    flamingo_kernel(nc, *args)
    return run_bass_kernel_spmd(nc, [arrays], core_ids=[0]).results[0]["out"]
```

```python
from contextlib import ExitStack

import concourse.bass as bass
from concourse import mybir

ALU = mybir.AluOpType
ACT = mybir.ActivationFunctionType
F32 = mybir.dt.float32
F32R = mybir.dt.float32r

EPS = 1e-5
CLIP = 11.0
EXP_LOW, EXP_HIGH = 1.6701700790245659e-05, 59874.14171519782


def flamingo_kernel(nc, x, ctx_in, g_xattn, g_ffn, cos, sin, lat_g, lat_b, ctx_g, ctx_b, w_q, w_kv, w_o, b_o,
                    w_1, b_1, w_2, b_2, w_r, b_r, out):
    P = 128
    B, N, D = x.shape
    S = ctx_in.shape[1]
    INNER = w_q.shape[1]
    HALF = cos.shape[1]
    DH = 2 * HALF
    E, _, HID = w_1.shape
    KT = D // P
    UNITS = INNER // (4 * DH)
    UW = 4 * DH
    ST = S // P
    NT = N // P
    CH = 4
    STEPS = 2 * CH
    BS = UNITS * STEPS
    PAIRS = 2 * UNITS
    MT = HID // P
    assert (P, KT, ST, NT, STEPS, DH, N) == (128, 2, 8, 4, ST, 64, 512)

    with ExitStack() as stack:
        def sb(name, shape, dt=F32):
            return stack.enter_context(nc.sbuf_tensor(name, [P] + shape, dt))

        def ps(name, width):
            return stack.enter_context(nc.psum_tensor(name, [P, width], F32))

        def sem(name):
            return stack.enter_context(nc.semaphore(name))

        big = [sb(f"big{i}", [4 * KT * 1024], F32R) for i in range(2)]
        wkv = big[0][:].rearrange("p (l k n) -> p l k n", l=2, k=KT)
        kst = big[1][:].rearrange("p (u h s) -> p u h s", u=2, h=4)
        acts = sb("acts", [8 * 1024], F32R)
        ctx_t = acts[:, 0:4 * S].rearrange("p (l k s) -> p l k s", l=2, k=KT)
        lat_t = acts[:, 4 * S:4 * S + 4 * N].rearrange("p (l k n) -> p l k n", l=2, k=KT)
        o_sp = acts[:, 4 * S + 4 * N:].rearrange("p (l q n) -> p l q n", l=2, q=2)
        x_t = acts[:].rearrange("p (t l k n) -> p t l k n", t=B, l=2, k=KT)
        q_hid = sb("q_hid", [8 * N], F32R)
        q_sp = q_hid[:].rearrange("p (r h l n) -> p r h l n", r=2, h=2, l=2)
        hid_sp = q_hid[:].rearrange("p (r l n) -> p r l n", r=4, l=2)
        wq = sb("wq", [2, KT * 4, 2, DH], F32R)
        wo = sb("wo", [2, 2, D], F32R)
        k_sp = sb("k_sp", [4, 2, DH], F32R)
        gb_sp = sb("gb_sp", [2, E * MT], F32R)

        val = sb("val", [2, ST, UW])
        wraw = val[:].rearrange("p u t n -> p (u t n)")
        prob = sb("prob", [2, 2, 2 * N])
        pall = prob[:].rearrange("p a h n -> p (a h n)")
        wkv_raw = pall.rearrange("p (u k w n) -> p u k w n", u=4, k=KT, w=2)
        acc = sb("acc", [2, 2 * N])
        xacc = sb("xacc", [B * NT, D])
        k_raw = sb("k_raw", [UW])
        rot_c = sb("rot_c", [UW])
        rot_s = sb("rot_s", [UW])
        k_rot = rot_c
        rows = sb("rows", [4, D])
        lat_r = sb("lat_r", [NT, D])
        c_aff = sb("c_aff", [KT, P])
        l_aff = sb("l_aff", [KT, 2 * P])
        recip = sb("recip", [N])
        cosb = sb("cosb", [ST, 2, HALF])
        sinb = sb("sinb", [ST, 2, HALF])
        w_raw = sb("w_raw", [2, UW])
        wq_twice = w_raw[:].rearrange("p k (h c) -> p (k h) c", c=DH).unsqueeze(2).to_broadcast([P, KT * 4, 2, DH])
        ident = sb("ident", [P])
        ones = sb("ones", [DH])
        mhalf = sb("mhalf", [8])
        eps = sb("eps", [8])
        c_bn = sb("c_bn", [4, 6])
        c_mv = sb("c_mv", [4, 2])
        c_rs = sb("c_rs", [4, 2])
        l_bn = sb("l_bn", [NT, 6])
        l_mv = sb("l_mv", [NT, 2])
        l_rs = sb("l_rs", [4, NT])
        f_stats = sb("f_stats", [B * NT * 10])
        affine = sb("affine", [4, KT])
        gates2 = sb("gates2", [4])
        b1t = sb("b1t", [E * MT])
        gb = sb("gb", [E * MT])
        wrt = sb("wrt", [KT, E])
        brb = sb("brb", [E])
        tgate = gates2[:, 2:3]
        fgate = gates2[:, 3:4]
        f_logit = rot_c[:, 0:64].rearrange("p (t e) -> p t e", e=E)
        f_tmp = rot_c[:, 64:128].rearrange("p (t e) -> p t e", e=E)
        f_rank = rot_c[:, 128:192].rearrange("p (t e) -> p t e", e=E)
        f_gate = rot_c[:, 192:256].rearrange("p (t e) -> p t e", e=E)
        f_max = rot_s[:, 0:16]
        f_sum = rot_s[:, 16:32]
        f_inv = rot_s[:, 32:48]
        f_bn = f_stats[:, 0:96].rearrange("p (t c) -> p t c", c=6)
        f_mv = f_stats[:, 96:128].rearrange("p (t c) -> p t c", c=2)
        f_rs = f_stats[:, 128:160].rearrange("p (a t) -> p a t", a=2)
        bo_b = c_aff[:].rearrange("p k n -> p (k n)")
        csum = recip[:, 0:D]
        f_rows = lat_r[:]
        b2b = rows[:]
        xt_raw = l_aff[:]
        hid = pall[:, 0:4 * N].rearrange("p (r n) -> p r n", r=4)

        sc = [ps("sc0", 2 * N), ps("sc1", 2 * N)]
        pv = ps("pv", N)
        kv = ps("kv", 2 * UW)
        tr = ps("tr", N)
        mi = ps("mi", N)
        hb = [sc[0][:, 0:N], sc[0][:, N:2 * N], kv[:], pv[:]]
        yb = [[sc[1][:, 0:N], sc[1][:, N:2 * N]], [tr[:], mi[:]]]

        ld_ctx = [sem(f"ld_ctx{i}") for i in range(4)]
        ld_x = [sem("ld_x0"), sem("ld_x1")]
        ld_w = [sem(f"ld_w{i}") for i in range(4)]
        ld_small = sem("ld_small")
        ld_wq = sem("ld_wq")
        ld_wo = sem("ld_wo")
        const = sem("const")
        wkv_h = sem("wkv_h")
        wkv_ready = sem("wkv_ready")
        tanh_ready = sem("tanh_ready")
        c_st = sem("c_st")
        c_ag = sem("c_ag")
        c_e1 = sem("c_e1")
        c_rstd = sem("c_rstd")
        c_norm = sem("c_norm")
        c_tr = sem("c_tr")
        c_affd = sem("c_affd")
        c_ready = sem("c_ready")
        l_st = sem("l_st")
        l_ag = sem("l_ag")
        l_ch = sem("l_ch")
        l_scale = sem("l_scale")
        l_norm = sem("l_norm")
        l_tr = sem("l_tr")
        l_affd = sem("l_affd")
        l_ready = sem("l_ready")
        wq_high = sem("wq_high")
        wq_ready = sem("wq_ready")
        wo_high = sem("wo_high")
        wo_ready = sem("wo_ready")
        kv_ready = sem("kv_ready")
        kraw_out = sem("kraw_out")
        kv_out = sem("kv_out")
        rot1 = sem("rot1")
        rot2 = sem("rot2")
        rot = sem("rot")
        k_high = sem("k_high")
        k_ready = sem("k_ready")
        k_tr = sem("k_tr")
        kst_ready = sem("kst_ready")
        q_mm = sem("q_mm")
        q_high = sem("q_high")
        q_ready = sem("q_ready")
        sc_ready = [sem("sc_ready0"), sem("sc_ready1")]
        exp_done = [sem("exp_done0"), sem("exp_done1")]
        clamped = [sem("clamped0"), sem("clamped1")]
        summed = [sem("summed0"), sem("summed1")]
        pv_done = sem("pv_done")
        den_ready = sem("den_ready")
        rec_done = sem("rec_done")
        o_norm = sem("o_norm")
        o_high = sem("o_high")
        o_ready = sem("o_ready")
        wo_mm = sem("wo_mm")
        wo_out = sem("wo_out")
        ld_bo = sem("ld_bo")
        ld_b2 = sem("ld_b2")
        f_ldw = [sem("f_ldw0"), sem("f_ldw1")]
        f_bo = sem("f_bo")
        f_stat = sem("f_stat")
        f_agg = sem("f_agg")
        f_eps = sem("f_eps")
        f_rstd = sem("f_rstd")
        f_norm = sem("f_norm")
        f_tr = sem("f_tr")
        f_raw = sem("f_raw")
        f_xready = sem("f_xready")
        f_lmm = sem("f_lmm")
        f_lout = sem("f_lout")
        f_chain = sem("f_chain")
        f_diff = sem("f_diff")
        f_exp = sem("f_exp")
        f_gates = sem("f_gates")
        gb_done = sem("gb_done")
        gbh = sem("gbh")
        gb_ready = sem("gb_ready")
        w_high = [sem("w_high0"), sem("w_high1")]
        w_ready = [sem("w_ready0"), sem("w_ready1")]
        h_mm = sem("h_mm")
        h_act = sem("h_act")
        h_high = sem("h_high")
        h_ready = sem("h_ready")
        y_mm = sem("y_mm")
        y_out = sem("y_out")
        cs_mm = sem("cs_mm")
        cs_chain = sem("cs_chain")
        fin = sem("fin")
        stored = sem("stored")

        def step_no(b, u, s):
            return b * BS + (u * STEPS + s)

        def tile_no(b, t):
            return b * ST + t

        def kv_no(b, u, t):
            return b * BS + (u * ST + t)

        def pair_no(b, p):
            return b * PAIRS + p

        QH = N // 2

        TURN = BS - ST - 5
        NORM, SCALE, LOAD = TURN - 1, TURN - 2, TURN - 4
        L_TURN = TURN + ST
        L_AGG, L_NORM = SCALE - NT - 1, SCALE

        def wait(eng, semaphore, count):
            if not (isinstance(count, int) and count <= 0):
                eng.wait_ge(semaphore, count)

        HALVES = 2 * B
        EARLY = (B - 1) * NT

        def half_at(u, s, last):
            return s if last and u == UNITS - 1 and s < HALVES - 2 else None

        def attention(eng, before, step):
            before()
            for s in range(STEPS):
                step(0, 0, s, False)
            with eng.Fori(0, B - 1) as b:
                for u in range(1, UNITS + 1):
                    for s in range(STEPS):
                        step(b + u // UNITS, u % UNITS, s, False)
            for u in range(1, UNITS):
                for s in range(STEPS):
                    step(B - 1, u, s, True)

        SLOTS = ST + 3

        def is_first(b, u):
            return isinstance(b, int) and b == 0 and u == 0

        def next_unit(b, u):
            return (b, u + 1) if u + 1 < UNITS else (b + 1, 0)

        def next_pair(b, p):
            return (b, p + 1) if p + 1 < PAIRS else (b + 1, 0)

        block = stack.enter_context(nc.Block())

        @block.sync
        def _(sp):
            def bcast(v):
                return v.rearrange("(a n) -> a n", a=1).to_broadcast([P, v.shape[0]])

            def load_ctx(b, t):
                wait(sp, c_tr, tile_no(b, t) - 3)
                src = ctx_in[b] if isinstance(b, int) else ctx_in[bass.ds(b, 1)].rearrange("a s d -> (a s) d")
                sp.dma_start(rows[:, t % 4, :], src[t * P:(t + 1) * P, :]).then_inc(ld_ctx[t % 4], 16)

            def load_wq(b, u):
                if isinstance(b, int) and b * UNITS + u == 1:
                    sp.wait_ge(wq_ready, 1)
                wait(sp, wo_ready, b * UNITS + u - 1)
                sp.dma_start(w_raw[:], w_q[:, u * UW:(u + 1) * UW].rearrange("(k p) n -> p k n", p=P)).then_inc(ld_wq, 16)

            def load_wo(b, u, last):
                if last and u == UNITS - 1:
                    sp.wait_ge(wo_ready, b * UNITS + u)
                else:
                    sp.wait_ge(wq_ready, b * UNITS + u + 2)
                sp.dma_start(w_raw[:], w_o[u * UW:(u + 1) * UW, :].rearrange("(q p) n -> p q n", p=P)).then_inc(ld_wo, 16)

            def load_wkv(u):
                for k in range(KT):
                    sp.dma_start(wkv_raw[:, u, k], w_kv[k * P:(k + 1) * P, :].rearrange("p (w n) -> p w n", w=2)
                                 [:, :, u * UW:(u + 1) * UW]).then_inc(ld_w[u], 16)

            def before():
                for t in range(4):
                    load_ctx(0, t)
                    if t == 1:
                        load_wkv(0)
                load_wq(0, 0)
                sp.dma_start(cosb[:, :, 0, :], cos.rearrange("(t p) c -> p t c", p=P)).then_inc(ld_small, 16)
                sp.dma_start(sinb[:, :, 1, :], sin.rearrange("(t p) c -> p t c", p=P)).then_inc(ld_small, 16)
                for u in range(1, UNITS):
                    load_wkv(u)
                    load_ctx(0, 3 + u)
                for t in range(3 + UNITS, ST):
                    load_ctx(0, t)

            def step(b, u, s, last):
                if s == 0:
                    nb, nu = next_unit(b, u)
                    if not (last and u == UNITS - 1):
                        load_wq(nb, nu)
                if s == 4:
                    load_wo(b, u, last)
                i = u * STEPS + s
                if not last and 0 <= i - LOAD < ST:
                    load_ctx(b + 1, i - LOAD)
                if last and i == STEPS:
                    sp.wait_ge(c_ready, B * ST)
                    sp.dma_start(bo_b, bcast(b_o)).then_inc(ld_bo, 16)
                    sp.dma_start(b2b, b_2.rearrange("(a e) n -> a e n", a=1).to_broadcast([P, E, D])).then_inc(ld_b2, 16)
                if last and i == BS - STEPS + 1:
                    sp.wait_ge(pv_done, (B - 1) * BS + BS - STEPS)
                    load_expert(0, 0, 0)
                    sp.wait_ge(w_ready[0], 1)
                    load_expert(0, 1, 0)

            def load_expert(e, half, slot):
                view = (w_1[e].rearrange("(k p) n -> p k n", p=P), w_2[e].rearrange("(m p) n -> p m n", p=P))[half]
                sp.dma_start(wraw[:, slot * 2048:(slot + 1) * 2048].rearrange("p (k n) -> p k n", k=view.shape[1]),
                             view).then_inc(f_ldw[half], 16)

            attention(sp, before, step)
            sp.wait_ge(w_ready[1], 1)
            load_expert(1, 0, 0)
            sp.wait_ge(pv_done, B * BS)
            load_expert(1, 1, 1)
            for e in range(2, E):
                for half in range(2):
                    sp.wait_ge(w_ready[half], e)
                    load_expert(e, half, half)
            for t in range(NT):
                sp.wait_ge(fin, t + 1)
                sp.dma_start(out[t].rearrange("(a p) d -> p a d", p=P), xacc[:, t * NT:(t + 1) * NT, :]).then_inc(stored, 16)
            sp.wait_ge(stored, 16 * NT)

        @block.gpsimd
        def _(pool):
            g = nc.gpsimd

            def ctx_scale(b, t):
                pool.wait_ge(c_ag, tile_no(b, t) + 1)
                g.tensor_tensor(c_rs[:, t % 4, 0:1], c_mv[:, t % 4, 1:2], eps[:, 0:1], ALU.add).then_inc(c_e1, 1)
                pool.wait_ge(c_e1, tile_no(b, t) + 1)
                g.tensor_tensor(c_rs[:, t % 4, 1:2], c_rs[:, t % 4, 0:1], mhalf[:, 0:1], ALU.pow).then_inc(c_rstd, 1)

            def lat_scale(b):
                pool.wait_ge(l_ag, b * NT + NT)
                v = l_mv[:, :, 1]
                e1, r, w, e2 = (l_rs[:, i, :] for i in range(4))
                n = [b * 6]

                def chain(ins):
                    n[0] = n[0] + 1
                    ins.then_inc(l_ch, 1)
                    pool.wait_ge(l_ch, n[0])

                chain(g.tensor_tensor(e1, v, eps[:, 0:NT], ALU.add))
                chain(g.tensor_tensor(r, e1, mhalf[:, 0:NT], ALU.pow))
                chain(g.tensor_tensor(w, r, r, ALU.mult))
                chain(g.tensor_tensor(w, w, v, ALU.mult))
                chain(g.tensor_tensor(w, w, eps[:, 0:NT], ALU.add))
                chain(g.tensor_tensor(e2, w, mhalf[:, 0:NT], ALU.pow))
                g.tensor_tensor(e1, e2, r, ALU.mult).then_inc(l_scale, 1)

            def wq_low(b, u):
                pool.wait_ge(wq_high, b * UNITS + u + 1)
                g.tensor_tensor(wq[:, 1], wq_twice, wq[:, 0].bitcast(F32), ALU.subtract).then_inc(wq_ready, 1)

            def wo_low(b, u):
                pool.wait_ge(wo_high, b * UNITS + u + 1)
                g.tensor_tensor(wo[:, 1], w_raw[:], wo[:, 0].bitcast(F32), ALU.subtract).then_inc(wo_ready, 1)

            def rotate(b, u, t):
                n = kv_no(b, u, t)
                kh = k_raw[:].rearrange("p (h a c) -> p h a c", h=4, a=2)
                pool.wait_ge(kraw_out, n + 1)
                g.tensor_tensor(rot_s[:].rearrange("p (h a c) -> p h a c", h=4, a=2), kh[:, :, ::-1, :],
                                sinb[:, t].unsqueeze(1).to_broadcast([P, 4, 2, HALF]), ALU.mult).then_inc(rot2, 1)
                pool.wait_ge(rot1, n + 1)
                pool.wait_ge(rot2, n + 1)
                g.tensor_tensor(k_rot[:], rot_c[:], rot_s[:], ALU.add).then_inc(rot, 1)
                pool.wait_ge(k_high, n + 1)
                g.tensor_tensor(k_sp[:, :, 1, :], k_rot[:].rearrange("p (h c) -> p h c", h=4),
                                k_sp[:, :, 0, :].bitcast(F32), ALU.subtract).then_inc(k_ready, 1)

            def rows_scale(t):
                pool.wait_ge(f_agg, NT * (t + 1))
                sl = slice(NT * t, NT * (t + 1))
                g.tensor_tensor(f_rs[:, 0, sl], f_mv[:, sl, 1], eps[:, 0:NT], ALU.add).then_inc(f_eps, 1)
                pool.wait_ge(f_eps, t + 1)
                g.tensor_tensor(f_rs[:, 1, sl], f_rs[:, 0, sl], mhalf[:, 0:NT], ALU.pow).then_inc(f_rstd, 1)

            def x_low(hf):
                pool.wait_ge(f_raw, hf + 1)
                t, sl = hf // 2, slice((hf % 2) * QH, (hf % 2 + 1) * QH)
                g.tensor_tensor(x_t[:, t, 1, :, sl], xt_raw, x_t[:, t, 0, :, sl].bitcast(F32), ALU.subtract).then_inc(f_xready, 1)

            def w_low(e, half, slot):
                pool.wait_ge(w_high[half], e + 1)
                w = big[e % 2][:, half * 4096:(half + 1) * 4096].rearrange("p (l n) -> p l n", l=2)
                g.tensor_tensor(w[:, 1, :], wraw[:, slot * 2048:(slot + 1) * 2048], w[:, 0, :].bitcast(F32),
                                ALU.subtract).then_inc(w_ready[half], 1)

            def before():
                g.memset(ident[:], 0.0).then_inc(const, 1)
                g.memset(mhalf[:], -0.5).then_inc(const, 1)
                g.memset(eps[:], EPS).then_inc(const, 1)
                g.memset(ones[:], 1.0).then_inc(const, 1)
                pool.wait_ge(const, 4)
                g.affine_select(out=ident[:], in_=ident[:], compare_op=ALU.not_equal, fill=1.0, base=0,
                                pattern=[[-1, P]], channel_multiplier=1).then_inc(const, 1)
                for t in range(SLOTS):
                    if t < ST:
                        ctx_scale(0, t)
                    if t == 2:
                        lat_scale(0)
                    if t == 3:
                        wq_low(0, 0)
                        pool.wait_ge(const, 7)
                    if 0 <= t - 3 < ST:
                        rotate(0, 0, t - 3)

            def step(b, u, s, last):
                i = u * STEPS + s
                make = not (last and u == UNITS - 1)
                if make:
                    rotate(*next_unit(b, u), s)
                    if s == 3:
                        wq_low(*next_unit(b, u))
                if s == 7:
                    wo_low(b, u)
                if not last and 0 <= i - SCALE < ST:
                    ctx_scale(b + 1, i - SCALE)
                if not last and i == L_NORM - 1:
                    lat_scale(b + 1)
                if last and i in (STEPS + 5, STEPS + 9, STEPS + 13):
                    rows_scale((i - STEPS - 5) // NT)
                if half_at(u, s, last) is not None:
                    x_low(s)
                    if s in (4, 5):
                        w_low(0, s - 4, 0)

            attention(pool, before, step)

            rows_scale(B - 1)
            x_low(HALVES - 2)
            x_low(HALVES - 1)
            for e in range(1, E):
                for half in range(2):
                    w_low(e, half, half)

        @block.scalar
        def _(act):
            a = nc.scalar

            def bcast(v):
                return v.rearrange("(a n) -> a n", a=1).to_broadcast([P, v.shape[0]])

            def kst_out(b, u, t):
                act.wait_ge(k_tr, kv_no(b, u, t) + 1)
                a.activation(kst[:, u % 2, :, t * P:(t + 1) * P], tr[:].rearrange("p (h s) -> p h s", h=4),
                             ACT.Copy).then_inc(kst_ready, 1)

            def kv_evac(b, u, t):
                act.wait_ge(kv_ready, kv_no(b, u, t) + 1)
                wait(act, k_ready, kv_no(b, u, t))
                a.activation(k_raw[:], kv[:, 0:UW], ACT.Copy).then_inc(kraw_out, 1)
                a.activation(val[:, u % 2, t, :], kv[:, UW:2 * UW], ACT.Copy).then_inc(kv_out, 1)

            def ctx_affine(b, t, bank):
                act.wait_ge(c_tr, tile_no(b, t) + 1)
                wait(act, c_ready, tile_no(b, t))
                for dst in (ctx_t[:, 0, :, t * P:(t + 1) * P], c_aff):
                    for k in range(KT):
                        last = a.activation(dst[:, k, :], bank[:, k * P:(k + 1) * P], ACT.Identity,
                                            scale=affine[:, 2, k:k + 1], bias=affine[:, 3, k:k + 1])
                last.then_inc(c_affd, 1)

            def lat_affine(b, hf, bank):
                act.wait_ge(l_tr, b * 2 + hf + 1)
                wait(act, l_ready, b * 2 + hf)
                for dst in (lat_t[:, 0, :, hf * QH:(hf + 1) * QH], l_aff):
                    for k in range(KT):
                        last = a.activation(dst[:, k, :], bank[:, k * QH:(k + 1) * QH], ACT.Identity,
                                            scale=affine[:, 0, k:k + 1], bias=affine[:, 1, k:k + 1])
                last.then_inc(l_affd, 1)

            def k_round(b, u, t):
                wait(act, k_tr, kv_no(b, u, t))
                act.wait_ge(rot, kv_no(b, u, t) + 1)
                a.activation(k_sp[:, :, 0, :], k_rot[:].rearrange("p (h c) -> p h c", h=4), ACT.Copy).then_inc(k_high, 1)

            def o_round(b, p):
                act.wait_ge(o_norm, pair_no(b, p) + 1)
                a.activation(o_sp[:, 0, p % 2, :], recip[:], ACT.Copy).then_inc(o_high, 1)

            def wkv_round(u):
                act.wait_ge(ld_w[u], 16 * KT)
                for w in range(2):
                    last = a.activation(wkv[:, 0, :, w * INNER + u * UW:w * INNER + (u + 1) * UW], wkv_raw[:, u, :, w, :],
                                        ACT.Copy)
                last.then_inc(wkv_h, 1)

            def wq_round(b, u):
                act.wait_ge(ld_wq, (b * UNITS + u + 1) * 16)
                a.activation(wq[:, 0], wq_twice, ACT.Copy).then_inc(wq_high, 1)

            def wo_round(b, u):
                act.wait_ge(ld_wo, (b * UNITS + u + 1) * 16)
                a.activation(wo[:, 0], w_raw[:], ACT.Copy).then_inc(wo_high, 1)

            def q_round(b, p, h):
                act.wait_ge(q_mm, pair_no(b, p) * 2 + h + 1)
                a.activation(q_sp[:, p % 2, h, 0, :], mi[:], ACT.Copy).then_inc(q_high, 1)

            def exps(b, u, s, h):
                act.wait_ge(sc_ready[h], step_no(b, u, s) + 1)
                c, q = s % CH, pair_no(b, u * 2 + s // CH)
                wait(act, summed[h], q * 4 + (-2, -1, 1, 1)[c])
                a.activation(prob[:, s % 2, h, :], sc[h][:], ACT.Exp, scale=DH ** -0.5).then_inc(exp_done[h], 1)

            def x_out(hf):
                act.wait_ge(f_tr, hf + 1)
                wait(act, f_xready, hf)
                wait(act, f_lmm, hf)
                t, sl = hf // 2, slice((hf % 2) * QH, (hf % 2 + 1) * QH)
                src = tr[:].rearrange("p (k n) -> p k n", k=KT)
                a.activation(x_t[:, t, 0, :, sl], src, ACT.Copy)
                a.activation(xt_raw, src, ACT.Copy).then_inc(f_raw, 1)

            def w_round(half):
                act.wait_ge(f_ldw[half], 16)
                a.activation(big[0][:, half * 4096:half * 4096 + 2048], wraw[:, 0:2048], ACT.Copy).then_inc(w_high[half], 1)

            def before():
                act.dma_start(xacc[:, 0:NT, :], x[0].rearrange("(a p) d -> p a d", p=P)).then_inc(ld_x[0], 16)
                for i, v in enumerate((lat_g, lat_b, ctx_g, ctx_b)):
                    with nc.allow_non_contiguous_dma(reason="four small vectors"):
                        act.dma_start(affine[:, i, :], v.rearrange("(k p) -> p k", p=P)).then_inc(ld_small, 16)
                with nc.allow_non_contiguous_dma(reason="small vectors of the experts"):
                    act.dma_start(b1t[:], b_1.rearrange("e (m p) -> p (e m)", p=P)).then_inc(ld_small, 16)
                    act.dma_start(wrt[:], w_r.rearrange("(k p) e -> p k e", p=P)).then_inc(ld_small, 16)
                act.dma_start(brb[:], bcast(b_r)).then_inc(ld_small, 16)
                act.dma_start(gates2[:, 0:1], bcast(g_xattn)).then_inc(ld_small, 16)
                act.dma_start(gates2[:, 1:2], bcast(g_ffn)).then_inc(ld_small, 16)
                for t in range(1, B):
                    act.dma_start(xacc[:, t * NT:(t + 1) * NT, :], x[t].rearrange("(a p) d -> p a d", p=P)).then_inc(ld_x[1], 16)
                act.wait_ge(ld_small, 16 * 11)
                a.activation(gates2[:, 2:4], gates2[:, 0:2], ACT.Tanh).then_inc(tanh_ready, 1)
                for t in range(SLOTS):
                    if 0 <= t - 1 < UNITS:
                        wkv_round(t - 1)
                    if t == 2:
                        wq_round(0, 0)
                    if 0 <= t - 3 < ST:
                        kv_evac(0, 0, t - 3)
                    if 0 <= t - 4 < ST - 1:
                        kst_out(0, 0, t - 4)
                    if 0 <= t - 1 < ST:
                        ctx_affine(0, t - 1, sc[0][:, ((t - 1) % 2) * N:((t - 1) % 2 + 1) * N])
                    if t == 4:
                        for hf in range(2):
                            lat_affine(0, hf, sc[1][:, hf * N:(hf + 1) * N])
                    if 0 <= t - 6 < 2:
                        q_round(0, 0, t - 6)
                    if 0 <= t - 3 < ST:
                        k_round(0, 0, t - 3)

            def step(b, u, s, last):
                i = u * STEPS + s
                p, c = u * 2 + s // CH, s % CH
                make = not (last and u == UNITS - 1)
                exps(b, u, s, 0)
                exps(b, u, s, 1)
                if make:
                    kv_evac(*next_unit(b, u), s)
                if s == 0:
                    kst_out(b, u, ST - 1)
                elif make:
                    kst_out(*next_unit(b, u), s - 1)
                if c == 1 and not (is_first(b, u) and s == 1):
                    o_round(*((b, p - 1) if p else (b - 1, PAIRS - 1)))
                if s == 3 and make:
                    wq_round(*next_unit(b, u))
                if s == 7:
                    wo_round(b, u)
                if make:
                    k_round(*next_unit(b, u), s)
                if not last and 0 <= i - TURN < ST:
                    ctx_affine(b + 1, i - TURN, tr)
                if not last and 0 <= i - L_TURN < 2:
                    lat_affine(b + 1, i - L_TURN, tr)
                if c in (1, 2) and not (last and p == PAIRS - 1):
                    q_round(*next_pair(b, p), c - 1)

                if half_at(u, s, last) is not None:
                    x_out(s)
                    if s in (3, 5):
                        w_round((s - 3) // 2)

            attention(act, before, step)

            def gelu(n, e, m):
                act.wait_ge(h_mm, n + 1)
                if not (isinstance(n, int) and n < 4):
                    act.wait_ge(h_ready, n - 3)
                a.activation(hid[:, m % 4, :], hb[m % 4], ACT.Gelu, bias=b1t[:, e * MT + m:e * MT + m + 1]).then_inc(h_act, 1)

            a.activation(gb[:], b1t[:], ACT.Gelu).then_inc(gb_done, 1)
            for n in range(B * MT):
                gelu(n, 0, n % MT)
                if n == 0:
                    o_round(B - 1, PAIRS - 1)
                if n == 6:
                    x_out(HALVES - 2)
                if n == 7:
                    x_out(HALVES - 1)
                if n == MT + 4:
                    act.wait_ge(f_diff, 1)
                    a.activation(f_tmp, f_logit, ACT.Exp).then_inc(f_exp, 1)
            for e in range(1, E):
                with act.Fori(0, B) as t:
                    for m in range(MT):
                        gelu(t * MT + (e * B * MT + m), e, m)

        @block.vector
        def _(dve):
            v = nc.vector

            def ctx_stats(b, t):
                dve.wait_ge(ld_ctx[t % 4], b * (16 * ST // 4) + 16 * (t // 4 + 1))
                v.bn_stats(c_bn[:, t % 4, :], rows[:, t % 4, :]).then_inc(c_st, 1)

            def ctx_aggregate(b, t):
                v.bn_aggr(c_mv[:, t % 4, :], c_bn[:, t % 4, :]).then_inc(c_ag, 1)

            def ctx_norm(b, t):
                dve.wait_ge(c_rstd, tile_no(b, t) + 1)
                v.tensor_scalar(rows[:, t % 4, :], rows[:, t % 4, :], c_mv[:, t % 4, 0:1], c_rs[:, t % 4, 1:2],
                                ALU.subtract, ALU.mult).then_inc(c_norm, 1)

            def ctx_low(b, t):
                dve.wait_ge(c_affd, tile_no(b, t) + 1)
                v.tensor_tensor(ctx_t[:, 1, :, t * P:(t + 1) * P], c_aff[:], ctx_t[:, 0, :, t * P:(t + 1) * P].bitcast(F32),
                                ALU.subtract).then_inc(c_ready, 1)

            def lat_stats(b, t):
                first = isinstance(b, int) and b == 0
                dve.wait_ge(ld_x[0 if first else 1], 16 if first else 16 * (B - 1))
                row = xacc[:, t, :] if isinstance(b, int) else xacc[:, bass.ds(b * NT + t, 1), :].rearrange("p a d -> p (a d)")
                v.bn_stats(l_bn[:, t, :], row).then_inc(l_st, 1)

            def lat_aggregate(b, t):
                v.bn_aggr(l_mv[:, t, :], l_bn[:, t, :]).then_inc(l_ag, 1)

            def lat_norm(b, t):
                dve.wait_ge(l_scale, b + 1)
                row = xacc[:, t, :] if isinstance(b, int) else xacc[:, bass.ds(b * NT + t, 1), :].rearrange("p a d -> p (a d)")
                v.tensor_scalar(lat_r[:, t, :], row, l_mv[:, t, 0:1], l_rs[:, 0, t:t + 1],
                                ALU.subtract, ALU.mult).then_inc(l_norm, 1)

            def lat_low(b, hf):
                dve.wait_ge(l_affd, b * 2 + hf + 1)
                sl = slice(hf * QH, (hf + 1) * QH)
                v.tensor_tensor(lat_t[:, 1, :, sl], l_aff[:], lat_t[:, 0, :, sl].bitcast(F32),
                                ALU.subtract).then_inc(l_ready, 1)

            def wkv_low(u):
                dve.wait_ge(wkv_h, u + 1)
                for w in range(2):
                    cols = slice(w * INNER + u * UW, w * INNER + (u + 1) * UW)
                    last = v.tensor_tensor(wkv[:, 1, :, cols], wkv_raw[:, u, :, w, :], wkv[:, 0, :, cols].bitcast(F32),
                                           ALU.subtract)
                last.then_inc(wkv_ready, 1)

            def rot_cos(b, u, t):
                dve.wait_ge(kraw_out, kv_no(b, u, t) + 1)
                v.tensor_tensor(rot_c[:].rearrange("p (h c) -> p h c", h=4), k_raw[:].rearrange("p (h c) -> p h c", h=4),
                                cosb[:, t].rearrange("p a c -> p (a c)").unsqueeze(1).to_broadcast([P, 4, DH]),
                                ALU.mult).then_inc(rot1, 1)

            def q_low(b, p, h):
                dve.wait_ge(q_high, pair_no(b, p) * 2 + h + 1)
                v.tensor_tensor(q_sp[:, p % 2, h, 1, :], mi[:], q_sp[:, p % 2, h, 0, :].bitcast(F32),
                                ALU.subtract).then_inc(q_ready, 1)

            def clamp(b, u, s, h):
                dve.wait_ge(exp_done[h], step_no(b, u, s) + 1)
                v.tensor_scalar(prob[:, s % 2, h, :], prob[:, s % 2, h, :], EXP_LOW, EXP_HIGH,
                                ALU.max, ALU.min).then_inc(clamped[h], 1)

            def sums(b, u, s, h):
                c, q = s % CH, pair_no(b, u * 2 + s // CH)
                if c == 0:
                    return
                dve.wait_ge(clamped[h], step_no(b, u, s) + 1)
                if c == 1:
                    wait(dve, den_ready, q)
                    v.tensor_tensor(acc[:, h, :], prob[:, 0, h, :], prob[:, 1, h, :], ALU.add).then_inc(summed[h], 1)
                else:
                    dve.wait_ge(summed[h], q * 4 + c - 1)
                    v.tensor_tensor(acc[:, h, :], acc[:, h, :], prob[:, s % 2, h, :], ALU.add).then_inc(summed[h], 1)

            def fold(b, p, h):
                dve.wait_ge(summed[h], pair_no(b, p) * 4 + 3)
                v.tensor_tensor(acc[:, h, 0:N], acc[:, h, 0:N], acc[:, h, N:2 * N], ALU.add).then_inc(summed[h], 1)

            def reciprocals(b, p):
                dve.wait_ge(den_ready, pair_no(b, p) + 1)
                v.reciprocal(recip[:], mi[:]).then_inc(rec_done, 1)

            def normalise(b, p):
                dve.wait_ge(pv_done, (pair_no(b, p) + 1) * CH)
                dve.wait_ge(rec_done, pair_no(b, p) + 1)
                v.tensor_tensor(recip[:], pv[:], recip[:], ALU.mult).then_inc(o_norm, 1)

            def o_low(b, p):
                dve.wait_ge(o_high, pair_no(b, p) + 1)
                v.tensor_tensor(o_sp[:, 1, p % 2, :], recip[:], o_sp[:, 0, p % 2, :].bitcast(F32),
                                ALU.subtract).then_inc(o_ready, 1)

            def residual(b, u, hf):
                dve.wait_ge(wo_mm, (b * UNITS + u) * 2 + hf + 1)
                if isinstance(b, int):
                    dst = xacc[:, b * NT + 2 * hf:b * NT + 2 * hf + 2, :]
                else:
                    dst = xacc[:, bass.ds(b * NT + 2 * hf, 2), :]
                v.scalar_tensor_tensor(dst, mi[:].rearrange("p (a d) -> p a d", a=2), tgate, dst,
                                       ALU.mult, ALU.add).then_inc(wo_out, 1)

            def before():
                for t in range(SLOTS):
                    if t < ST:
                        ctx_stats(0, t)
                        dve.wait_ge(c_st, t + 1)
                        ctx_aggregate(0, t)
                    if t == 1:
                        for i in range(NT):
                            lat_stats(0, i)
                            dve.wait_ge(l_st, i + 1)
                            lat_aggregate(0, i)
                    if 0 <= t - 1 < ST:
                        ctx_norm(0, t - 1)
                    if 0 <= t - 2 < UNITS:
                        wkv_low(t - 2)
                    if t == 2:
                        dve.wait_ge(ld_small, 16 * 11)
                        v.tensor_copy(cosb[:, :, 1, :], cosb[:, :, 0, :]).then_inc(const, 1)
                        v.tensor_scalar(sinb[:, :, 0, :], sinb[:, :, 1, :], -1.0, None, ALU.mult).then_inc(const, 1)
                        dve.wait_ge(const, 7)
                    if 0 <= t - 2 < ST:
                        ctx_low(0, t - 2)
                    if t == 3:
                        for i in range(NT):
                            lat_norm(0, i)
                    if t == 5:
                        lat_low(0, 0)
                        lat_low(0, 1)
                    if 0 <= t - 7 < 2:
                        q_low(0, 0, t - 7)
                    if 0 <= t - 3 < ST:
                        rot_cos(0, 0, t - 3)
                dve.wait_ge(tanh_ready, 1)

            def step(b, u, s, last):
                i = u * STEPS + s
                p = u * 2 + s // CH
                c = s % CH
                make = not (last and u == UNITS - 1)
                last_pair = (b, p - 1) if p else (b - 1, PAIRS - 1)
                has_last = not (is_first(b, u) and s < CH)
                if c >= 2 and not (last and p == PAIRS - 1):
                    q_low(*next_pair(b, p), c - 2)
                if c == 1 and has_last:
                    normalise(*last_pair)
                ct, lt = i - SCALE, i - L_AGG
                if not last and 0 <= ct < ST:
                    dve.wait_ge(c_st, tile_no(b + 1, ct) + 1)
                if not last and 0 <= lt < NT:
                    dve.wait_ge(l_st, (b + 1) * NT + lt + 1)
                early = last and 0 <= i - STEPS - 1 < EARLY
                if early:
                    dve.wait_ge(f_stat, i - STEPS)
                clamp(b, u, s, 0)
                if early:
                    rows_aggregate(i - STEPS - 1)
                if not last and 0 <= ct < ST:
                    ctx_aggregate(b + 1, ct)
                if not last and 0 <= lt < NT:
                    lat_aggregate(b + 1, lt)
                clamp(b, u, s, 1)
                if make:
                    rot_cos(*next_unit(b, u), s)
                if not last and 0 <= i - TURN - 1 < ST:
                    ctx_low(b + 1, i - TURN - 1)
                if not last and 0 <= i - L_TURN - 1 < 2:
                    lat_low(b + 1, i - L_TURN - 1)
                sums(b, u, s, 0)
                if s in (2, 3) and not is_first(b, u):
                    residual(*((b, u - 1) if u else (b - 1, UNITS - 1)), s - 2)
                sums(b, u, s, 1)
                if c == CH - 1:
                    fold(b, p, 0)
                    fold(b, p, 1)
                if c == 0 and has_last:
                    reciprocals(*last_pair)
                if c == 1 and has_last:
                    o_low(*last_pair)
                if not last:
                    if 0 <= ct + 1 < ST:
                        ctx_stats(b + 1, ct + 1)
                    if 0 <= i - NORM < ST:
                        ctx_norm(b + 1, i - NORM)
                    if 0 <= lt + 1 < NT:
                        lat_stats(b + 1, lt + 1)
                    if 0 <= i - L_NORM < NT:
                        lat_norm(b + 1, i - L_NORM)

                if last and 0 <= i - STEPS < EARLY:
                    rows_stats(i - STEPS)
                hf = half_at(u, s, last)
                if hf is not None:
                    rows_norm(hf)
                if last and i == BS - 1:
                    logits(0, EARLY, kv)

            def rows_stats(j):
                wait(dve, ld_bo, 16)
                v.scalar_tensor_tensor(xacc[:, j, :], bo_b, tgate, xacc[:, j, :], ALU.mult, ALU.add).then_inc(f_bo, 1)
                dve.wait_ge(f_bo, j + 1)
                v.bn_stats(f_bn[:, j, :], xacc[:, j, :]).then_inc(f_stat, 1)

            def rows_aggregate(j):
                v.bn_aggr(f_mv[:, j, :], f_bn[:, j, :]).then_inc(f_agg, 1)

            def rows_norm(hf):
                dve.wait_ge(f_rstd, hf // 2 + 1)
                wait(dve, f_tr, hf - 1)
                for i in range(2):
                    j = 2 * hf + i
                    v.tensor_scalar(f_rows[:, j % 4, :], xacc[:, j, :], f_mv[:, j, 0:1], f_rs[:, 1, j:j + 1],
                                    ALU.subtract, ALU.mult).then_inc(f_norm, 1)

            def logits(lo, hi, bank):
                if lo == 0:
                    dve.wait_ge(k_ready, B * BS)
                dve.wait_ge(f_lmm, hi // 2)
                v.tensor_tensor(f_logit[:, lo:hi, :], bank[:, 0:(hi - lo) * E].rearrange("p (t e) -> p t e", e=E),
                                brb[:].unsqueeze(1).to_broadcast([P, hi - lo, E]), ALU.add).then_inc(f_lout, 1)

            attention(dve, before, step)

            w1v = [big[i][:, 0:4096].rearrange("p (l n) -> p l n", l=2) for i in range(2)]
            w2v = [big[i][:, 4096:8192].rearrange("p (l n) -> p l n", l=2) for i in range(2)]

            def split_high(e, half):
                w = (w1v, w2v)[half][e % 2]
                dve.wait_ge(f_ldw[half], 16 * (e + 1))
                v.tensor_copy(w[:, 0, :], wraw[:, half * 2048:half * 2048 + 2048]).then_inc(w_high[half], 1)

            n_chain = [0]

            def chain(ins):
                n_chain[0] += 1
                ins.then_inc(f_chain, 1)
                dve.wait_ge(f_chain, n_chain[0])

            R = B * NT

            def gates_rank(j):
                if j == 0:
                    dve.wait_ge(f_lout, 2)
                    chain(v.tensor_reduce(f_max, f_logit, mybir.AxisListType.X, ALU.max))
                to = f_rank if j == 0 else f_gate
                for lo, hi, op in ((0, j + 1, ALU.is_gt), (j + 1, E, ALU.is_ge)):
                    if hi > lo:
                        chain(v.tensor_tensor(to[:, :, lo:hi], f_logit[:, :, j:j + 1].to_broadcast([P, R, hi - lo]),
                                              f_logit[:, :, lo:hi], op))
                if j:
                    chain(v.tensor_tensor(f_rank, f_rank, f_gate, ALU.add))
                if j == E - 1:
                    v.tensor_tensor(f_logit, f_logit, f_max.unsqueeze(2).to_broadcast([P, R, E]),
                                    ALU.subtract).then_inc(f_diff, 1)

            def gates_last():
                dve.wait_ge(f_exp, 1)
                chain(v.scalar_tensor_tensor(f_gate, f_rank, 2.0, f_tmp, ALU.is_lt, ALU.mult))
                chain(v.tensor_reduce(f_sum, f_gate, mybir.AxisListType.X, ALU.add))
                chain(v.reciprocal(f_inv, f_sum))
                chain(v.scalar_tensor_tensor(f_gate, f_gate, fgate, f_inv.unsqueeze(2).to_broadcast([P, R, E]),
                                             ALU.mult, ALU.mult))

            def b2_sum():
                dve.wait_ge(ld_b2, 16)
                chain(v.tensor_tensor(csum, b2b[:, 0, :], b2b[:, 1, :], ALU.add))
                for e in range(2, E):
                    chain(v.tensor_tensor(csum, csum, b2b[:, e, :], ALU.add))

            def gelu_b1():
                dve.wait_ge(gb_done, 1)
                v.tensor_copy(gb_sp[:, 0, :], gb[:]).then_inc(gbh, 1)
                dve.wait_ge(gbh, 1)
                v.tensor_tensor(gb_sp[:, 1, :], gb[:], gb_sp[:, 0, :].bitcast(F32), ALU.subtract).then_inc(gb_ready, 1)

            def biases(e):
                dve.wait_ge(cs_mm, e)
                chain(v.tensor_tensor(csum, hb[3][:, 0:D], csum, ALU.add))
                if e == E - 1:
                    chain(v.tensor_scalar(csum, csum, fgate, None, ALU.mult))

            def hidden(n, e, m):
                dve.wait_ge(h_act, n + 1)
                wait(dve, y_mm, n - 3)
                c = gb[:, e * MT + m:e * MT + m + 1]
                v.tensor_scalar(hid_sp[:, m % 4, 0, :], hid[:, m % 4, :], c, None, ALU.subtract).then_inc(h_high, 1)
                dve.wait_ge(h_high, n + 1)
                v.scalar_tensor_tensor(hid_sp[:, m % 4, 1, :], hid[:, m % 4, :], c, hid_sp[:, m % 4, 0, :].bitcast(F32),
                                       ALU.subtract, ALU.subtract).then_inc(h_ready, 1)

            def combine(e, t, parity):
                dve.wait_ge(y_mm, (t + e * B + 1) * MT)
                for i in range(NT):
                    if isinstance(t, int):
                        row, gate = xacc[:, t * NT + i, :], f_gate[:, t * NT + i, e:e + 1]
                    else:
                        row = xacc[:, bass.ds(t * NT + i, 1), :].rearrange("p a d -> p (a d)")
                        gate = f_gate[:, bass.ds(t * NT + i, 1), e:e + 1].rearrange("p a d -> p (a d)")
                    v.scalar_tensor_tensor(row, yb[parity][i // 2][:, (i % 2) * D:(i % 2 + 1) * D], gate, row,
                                           ALU.mult, ALU.add).then_inc(y_out, 1)
                if e == E - 1:
                    dve.wait_ge(y_out, (t + e * B + 1) * NT)
                    dst = xacc[:, bass.ds(t * NT, NT), :]
                    v.tensor_tensor(dst, dst, csum.unsqueeze(1).to_broadcast([P, NT, D]), ALU.add).then_inc(fin, 1)

            reciprocals(B - 1, PAIRS - 1)
            normalise(B - 1, PAIRS - 1)
            for n in range(B * MT):
                t, m = n // MT, n % MT
                hidden(n, 0, m)
                if t == 0:
                    if m == 0:
                        o_low(B - 1, PAIRS - 1)
                    if m in (1, 2):
                        residual(B - 1, UNITS - 1, m - 1)
                    if m == 3:
                        for i in range(NT):
                            rows_stats(EARLY + i)
                        for i in range(NT):
                            dve.wait_ge(f_stat, EARLY + i + 1)
                            rows_aggregate(EARLY + i)
                    if m == 4:
                        rows_norm(HALVES - 2)
                    if m == 5:
                        rows_norm(HALVES - 1)
                    if m == 7:
                        logits(EARLY, B * NT, mi)
                if t == 1:
                    if m < E:
                        gates_rank(m)
                    if m == 5:
                        gates_last()
                    if m == 6:
                        combine(0, 0, 0)
                if t == 2:
                    if m == 0:
                        b2_sum()
                    if m == 1:
                        gelu_b1()
                    if m in (3, 5):
                        split_high(1, (m - 3) // 2)
                if t and m == MT - 1:
                    combine(0, t, t % 2)
            for e in range(1, E):
                biases(e)
                if e + 1 < E:
                    split_high(e + 1, 0)
                    split_high(e + 1, 1)
                with dve.Fori(0, B // 2) as d:
                    for r in range(2):
                        for m in range(MT):
                            hidden((d * 2 + r + e * B) * MT + m, e, m)
                        combine(e, d * 2 + r, r)

        @block.tensor
        def _(pe):
            mm = nc.tensor.matmul

            def three(dst, lhs, rhs, start, stop, **kw):
                mm(dst, lhs(0), rhs(0), start=start, stop=False, **kw)
                mm(dst, lhs(0), rhs(1), start=False, stop=False, **kw)
                return mm(dst, lhs(1), rhs(0), start=False, stop=stop, **kw)

            def ctx_turn(b, t, bank):
                pe.wait_ge(c_norm, tile_no(b, t) + 1)
                for k in range(KT):
                    last = nc.tensor.transpose(bank[:, k * P:(k + 1) * P], rows[:, t % 4, k * P:(k + 1) * P], ident[:])
                last.then_inc(c_tr, 1)

            def lat_turn(b, hf, bank):
                pe.wait_ge(l_norm, b * NT + 2 * hf + 2)
                for i in range(2):
                    for k in range(KT):
                        last = nc.tensor.transpose(bank[:, k * QH + i * P:k * QH + (i + 1) * P],
                                                   lat_r[:, 2 * hf + i, k * P:(k + 1) * P], ident[:])
                last.then_inc(l_tr, 1)

            def q_make(b, p, h):
                pe.wait_ge(l_ready, 2 * b + 2)
                pe.wait_ge(wq_ready, b * UNITS + p // 2 + 1)
                c = (p % 2) * 2 + h
                for k in range(KT):
                    last = three(mi[:], lambda l: wq[:, l, k * 4 + c].rearrange("p a c -> p (a c)"),
                                 lambda l: lat_t[:, l, k, :], k == 0, k == KT - 1)
                last.then_inc(q_mm, 1)

            def kv_make(b, u, t):
                pe.wait_ge(c_ready, tile_no(b, t) + 1)
                wait(pe, kv_out, kv_no(b, u, t))
                for k in range(KT):
                    last = three(kv[:].rearrange("p (w n) -> p w n", w=2), lambda l: ctx_t[:, l, k, t * P:(t + 1) * P],
                                 lambda l: wkv[:, l, k, :].rearrange("p (w n) -> p w n", w=2)[:, :, u * UW:(u + 1) * UW],
                                 k == 0, k == KT - 1)
                last.then_inc(kv_ready, 1)

            def k_turn(b, u, t):
                pe.wait_ge(k_ready, kv_no(b, u, t) + 1)
                wait(pe, kst_ready, kv_no(b, u, t))
                for h in range(4):
                    last = nc.tensor.transpose(tr[:, h * P:(h + 1) * P],
                                               k_sp[:, h].rearrange("p l c -> p (l c)").bitcast(F32), ident[:])
                last.then_inc(k_tr, 1)

            def score(b, u, s, h):
                c, j, p = s % CH, s // CH, u * 2 + s // CH
                if h == 0:
                    pe.wait_ge(kst_ready, kv_no(b, u, 2 * c + 1) + 1)
                if c == 0:
                    pe.wait_ge(q_ready, pair_no(b, p) * 2 + h + 1)
                wait(pe, exp_done[h], step_no(b, u, s))
                for i in range(2):
                    t = 2 * c + i
                    for l in range(2):
                        last = mm(sc[h][:, i * N:(i + 1) * N], kst[:, u % 2, 2 * j + h, t * P:(t + 1) * P],
                                  q_sp[:, j, h, l, :], start=l == 0, stop=l == 1)
                last.then_inc(sc_ready[h], 1)

            def values(b, u, s):
                c, j, p = s % CH, s // CH, u * 2 + s // CH
                if c == 0:
                    wait(pe, o_norm, pair_no(b, p))
                for h in range(2):
                    pe.wait_ge(clamped[h], step_no(b, u, s) + 1)
                for i in range(2):
                    for h in range(2):
                        last = mm(pv[h * DH:(h + 1) * DH, :], val[:, u % 2, 2 * c + i, (2 * j + h) * DH:(2 * j + h + 1) * DH],
                                  prob[:, s % 2, h, i * N:(i + 1) * N], start=c == 0 and i == 0, stop=c == CH - 1 and i == 1)
                last.then_inc(pv_done, 1)

            def denominators(b, p):
                for h in range(2):
                    pe.wait_ge(summed[h], (pair_no(b, p) + 1) * 4)
                    last = mm(mi[h * DH:(h + 1) * DH, :], ones[:], acc[:, h, 0:N], start=True, stop=True)
                last.then_inc(den_ready, 1)

            def project(b, u, hf):
                pe.wait_ge(o_ready, pair_no(b, 2 * u + 1) + 1)
                pe.wait_ge(wo_ready, b * UNITS + u + 1)
                for i in range(2):
                    for j in range(2):
                        last = three(mi[:, i * D:(i + 1) * D], lambda l: o_sp[:, l, j, (2 * hf + i) * P:(2 * hf + i + 1) * P],
                                     lambda l: wo[:, l, j, :], j == 0, j == 1)
                last.then_inc(wo_mm, 1)

            def x_turn(hf):
                pe.wait_ge(f_norm, 2 * hf + 2)
                for i in range(2):
                    for k in range(KT):
                        last = nc.tensor.transpose(tr[:, k * QH + i * P:k * QH + (i + 1) * P],
                                                   f_rows[:, (2 * hf + i) % 4, k * P:(k + 1) * P], ident[:])
                last.then_inc(f_tr, 1)

            def router(hf, bank, at):
                pe.wait_ge(f_raw, hf + 1)
                for i in range(2):
                    for k in range(KT):
                        last = mm(bank[:, (at + i) * E:(at + i + 1) * E], xt_raw[:, k, i * P:(i + 1) * P], wrt[:, k, :],
                                  start=k == 0, stop=k == KT - 1)
                last.then_inc(f_lmm, 1)

            def before():
                pe.wait_ge(const, 5)
                for t in range(SLOTS):
                    if 0 <= t - 3 < ST:
                        pe.wait_ge(wkv_ready, 1)
                        kv_make(0, 0, t - 3)
                    if 0 <= t - 4 < ST - 1:
                        k_turn(0, 0, t - 4)
                    if 0 <= t - 1 < ST:
                        wait(pe, c_affd, t - 2)
                        ctx_turn(0, t - 1, sc[0][:, ((t - 1) % 2) * N:((t - 1) % 2 + 1) * N])
                    if t == 4:
                        for hf in range(2):
                            lat_turn(0, hf, sc[1][:, hf * N:(hf + 1) * N])
                    if 0 <= t - 6 < 2:
                        wait(pe, q_ready, t - 6)
                        q_make(0, 0, t - 6)
                pe.wait_ge(wkv_ready, UNITS)

            def step(b, u, s, last):
                i = u * STEPS + s
                p, c = u * 2 + s // CH, s % CH
                make = not (last and u == UNITS - 1)
                nb, nu = next_unit(b, u)
                score(b, u, s, 0)
                score(b, u, s, 1)
                if make:
                    kv_make(nb, nu, s)
                if s == 0 or make:
                    if not last and 0 <= i - TURN - 1 < ST:
                        pe.wait_ge(c_affd, tile_no(b + 1, i - TURN - 1) + 1)
                    if not last and 0 <= i - L_TURN - 1 < 2:
                        pe.wait_ge(l_affd, 2 * (b + 1) + i - L_TURN)
                    k_turn(*((nb, nu, s - 1) if s else (b, u, ST - 1)))
                if c == 0 and not (is_first(b, u) and s == 0):
                    pe.wait_ge(q_ready, pair_no(b, p) * 2 + 2)
                    wait(pe, wo_out, (b * UNITS + u) * 2 - (2 if s == 0 else 0))
                    denominators(*((b, p - 1) if p else (b - 1, PAIRS - 1)))
                if s in (2, 3) and not is_first(b, u):
                    if not (last and p == PAIRS - 1):
                        pe.wait_ge(q_ready, pair_no(b, p + 1) * 2 + c - 1)
                    wait(pe, wo_out, (b * UNITS + u) * 2 + s - 4)
                    project(*((b, u - 1) if u else (b - 1, UNITS - 1)), s - 2)
                if not (is_first(b, u) and s == 0):
                    values(*((b, u, s - 1) if s else (b, u - 1, STEPS - 1) if u else (b - 1, UNITS - 1, STEPS - 1)))
                if c in (1, 2) and not (last and p == PAIRS - 1):
                    wait(pe, rec_done, pair_no(b, p))
                    if s == 2:
                        wait(pe, wo_out, (b * UNITS + u) * 2 - 1)
                    if c == 2:
                        pe.wait_ge(q_ready, pair_no(b, p + 1) * 2 + 1)
                    q_make(*next_pair(b, p), c - 1)
                if not last and TURN <= i < L_TURN + 2:
                    pe.wait_ge(kst_ready, kv_no(nb, nu, s - 1) + 1 if s else kv_no(b, u, ST - 1) + 1)
                    if i < L_TURN:
                        ctx_turn(b + 1, i - TURN, tr)
                    else:
                        lat_turn(b + 1, i - L_TURN, tr)
                if half_at(u, s, last) is not None:
                    if s == 0:
                        pe.wait_ge(kst_ready, B * BS)
                        pe.wait_ge(kv_out, B * BS)
                    else:
                        router(s - 1, kv, 2 * (s - 1))
                    x_turn(s)
                if last and i == BS - 2:
                    router(HALVES - 3, kv, 2 * (HALVES - 3))

            attention(pe, before, step)
            values(B - 1, UNITS - 1, STEPS - 1)

            w1v = [big[i][:, 0:4096].rearrange("p (l k n) -> p l k n", l=2, k=KT) for i in range(2)]
            w2v = [big[i][:, 4096:8192].rearrange("p (l m n) -> p l m n", l=2, m=MT) for i in range(2)]

            def hidden(n, e, t, m):
                wait(pe, h_act, n - 3)
                x_at = x_t[:, t] if isinstance(t, int) else x_t[:, bass.ds(t, 1)].rearrange("p a l k n -> p (a l) k n")
                for k in range(KT):
                    last = three(hb[m % 4], lambda l: w1v[e % 2][:, l, k, m * P:(m + 1) * P], lambda l: x_at[:, l, k, :],
                                 k == 0, k == KT - 1)
                last.then_inc(h_mm, 1)

            def outputs(n, e, t, m, parity):
                pe.wait_ge(h_ready, n + 1)
                if m == 0:
                    wait(pe, y_out, (t + e * B - 1) * NT)
                for i in range(NT):
                    last = three(yb[parity][i // 2][:, (i % 2) * D:(i % 2 + 1) * D],
                                 lambda l: hid_sp[:, m % 4, l, i * P:(i + 1) * P],
                                 lambda l: w2v[e % 2][:, l, m, :], m == 0 and i % 2 == 0, m == MT - 1 and i % 2 == 1,
                                 skip_group_check=True)
                last.then_inc(y_mm, 1)

            def block_of(e, t, parity, behind=lambda m: None):
                for m in range(3):
                    hidden((t + e * B) * MT + m, e, t, m)
                    behind(m - 3)
                for m in range(MT):
                    outputs((t + e * B) * MT + m, e, t, m, parity)
                    if m + 3 < MT:
                        hidden((t + e * B) * MT + m + 3, e, t, m + 3)
                    behind(m)

            def first_block(m):
                if m == -3:
                    denominators(B - 1, PAIRS - 1)
                    pe.wait_ge(f_lout, 1)
                    pe.wait_ge(w_ready[1], 1)
                if m == 0:
                    pe.wait_ge(rec_done, B * PAIRS)
                    project(B - 1, UNITS - 1, 0)
                if m == 1:
                    pe.wait_ge(wo_out, B * UNITS * 2 - 1)
                    project(B - 1, UNITS - 1, 1)
                if m == 4:
                    x_turn(HALVES - 2)
                if m == 5:
                    pe.wait_ge(wo_out, B * UNITS * 2)
                    router(HALVES - 2, mi, 0)
                    x_turn(HALVES - 1)
                if m == MT - 1:
                    router(HALVES - 1, mi, 2)

            def second_block(m):
                if m == -1:
                    pe.wait_ge(f_xready, HALVES)
                    pe.wait_ge(f_lout, 2)

            def biases(e, start):
                for m in range(MT):
                    last = three(hb[3][:, 0:D], lambda l: gb_sp[:, l, e * MT + m:e * MT + m + 1].to_broadcast([P, P]),
                                 lambda l: w2v[e % 2][:, l, m, :], start and m == 0, e > 0 and m == MT - 1)
                return last

            pe.wait_ge(f_xready, HALVES - 2)
            pe.wait_ge(w_ready[0], 1)
            block_of(0, 0, 0, first_block)
            for t in range(1, B):
                block_of(0, t, t % 2, second_block if t == 1 else lambda m: None)
            pe.wait_ge(gb_ready, 1)
            for e in range(1, E):
                pe.wait_ge(w_ready[0], e + 1)
                pe.wait_ge(w_ready[1], e + 1)
                pe.wait_ge(h_act, e * B * MT)
                if e == 1:
                    biases(0, True)
                biases(e, e > 1).then_inc(cs_mm, 1)
                with pe.Fori(0, B // 2) as d:
                    for r in range(2):
                        block_of(e, d * 2 + r, r)


INPUTS = ["x", "ctx_1024", "g_xattn", "g_ffn", "L0_xattn_cos", "L0_xattn_sin", "L0_xattn_ln_lat_g", "L0_xattn_ln_lat_b",
          "L0_xattn_ln_ctx_g", "L0_xattn_ln_ctx_b", "L0_xattn_Wq", "L0_xattn_Wkv", "L0_xattn_Wo", "L0_xattn_bo",
          "L0_ffn_w1", "L0_ffn_b1", "L0_ffn_w2", "L0_ffn_b2", "L0_ffn_wr", "L0_ffn_br"]


def kernel(**inputs):
    import numpy as np
    import concourse.bacc as bacc
    from concourse.bass_utils import run_bass_kernel_spmd

    nc = bacc.Bacc("TRN2", target_bir_lowering=False, num_devices=1)
    arrays, args = {}, []
    for name in INPUTS:
        value = np.ascontiguousarray(inputs[name])
        arrays[f"in_{name}"] = value
        args.append(nc.dram_tensor(f"in_{name}", value.shape, mybir.dt.from_np(value.dtype), kind="ExternalInput").ap())
    shape = inputs["x"].shape
    args.append(nc.dram_tensor("out", shape, F32, kind="ExternalOutput").ap())
    flamingo_kernel(nc, *args)
    return run_bass_kernel_spmd(nc, [arrays], core_ids=[0]).results[0]["out"]
```

```python
from contextlib import ExitStack

import concourse.bass as bass
from concourse import mybir

ALU = mybir.AluOpType
ACT = mybir.ActivationFunctionType
F32 = mybir.dt.float32
F32R = mybir.dt.float32r

EPS = 1e-5
CLIP = 11.0
EXP_LOW, EXP_HIGH = 1.6701700790245659e-05, 59874.14171519782


def flamingo_kernel(nc, x, ctx_in, g_xattn, g_ffn, cos, sin, lat_g, lat_b, ctx_g, ctx_b, w_q, w_kv, w_o, b_o,
                    w_1, b_1, w_2, b_2, w_r, b_r, out):
    P = 128
    B, N, D = x.shape
    S = ctx_in.shape[1]
    INNER = w_q.shape[1]
    HALF = cos.shape[1]
    DH = 2 * HALF
    E, _, HID = w_1.shape
    KT = D // P
    UNITS = INNER // (4 * DH)
    UW = 4 * DH
    ST = S // P
    NT = N // P
    CH = 4
    STEPS = 2 * CH
    BS = UNITS * STEPS
    PAIRS = 2 * UNITS
    MT = HID // P
    assert (P, KT, ST, NT, STEPS, DH, N) == (128, 2, 8, 4, ST, 64, 512)

    with ExitStack() as stack:
        def sb(name, shape, dt=F32):
            return stack.enter_context(nc.sbuf_tensor(name, [P] + shape, dt))

        def ps(name, width):
            return stack.enter_context(nc.psum_tensor(name, [P, width], F32))

        def sem(name):
            return stack.enter_context(nc.semaphore(name))

        big = [sb(f"big{i}", [4 * KT * 1024], F32R) for i in range(2)]
        wkv = big[0][:].rearrange("p (l k n) -> p l k n", l=2, k=KT)
        kst = big[1][:].rearrange("p (u h s) -> p u h s", u=2, h=4)
        acts = sb("acts", [8 * 1024], F32R)
        ctx_t = acts[:, 0:4 * S].rearrange("p (l k s) -> p l k s", l=2, k=KT)
        lat_t = acts[:, 4 * S:4 * S + 4 * N].rearrange("p (l k n) -> p l k n", l=2, k=KT)
        o_sp = acts[:, 4 * S + 4 * N:].rearrange("p (l q n) -> p l q n", l=2, q=2)
        x_t = acts[:].rearrange("p (t l k n) -> p t l k n", t=B, l=2, k=KT)
        q_hid = sb("q_hid", [8 * N], F32R)
        q_sp = q_hid[:].rearrange("p (r h l n) -> p r h l n", r=2, h=2, l=2)
        hid_sp = q_hid[:].rearrange("p (r l n) -> p r l n", r=4, l=2)
        q_pair = sb("q_pair", [2, N], F32R)
        wq = sb("wq", [2, KT, UW], F32R)
        wo = sb("wo", [2, 2, D], F32R)
        k_t = sb("k_t", [2, 2, UW], F32R)
        gb_sp = sb("gb_sp", [2, E * MT], F32R)

        val = sb("val", [2, ST, UW])
        wraw = val[:].rearrange("p u t n -> p (u t n)")
        prob = sb("prob", [2, 2, 2 * N])
        pall = prob[:].rearrange("p a h n -> p (a h n)")
        wkv_raw = pall.rearrange("p (u k w n) -> p u k w n", u=4, k=KT, w=2)
        acc = sb("acc", [2, 2 * N])
        xacc = sb("xacc", [B * NT, D])
        k_raw = sb("k_raw", [UW])
        rot_c = sb("rot_c", [UW])
        rot_s = sb("rot_s", [UW])
        k_rot = rot_c
        k_whole = sb("k_whole", [UW])
        rows = sb("rows", [4, D])
        lat_r = sb("lat_r", [NT, D])
        c_aff = sb("c_aff", [KT, P])
        l_aff = sb("l_aff", [KT, 2 * P])
        recip = sb("recip", [N])
        cosb = sb("cosb", [ST, HALF])
        sinb = sb("sinb", [ST, 2, HALF])
        w_raw = sb("w_raw", [2, UW])
        ident = sb("ident", [P])
        ones = sb("ones", [DH])
        mhalf = sb("mhalf", [8])
        eps = sb("eps", [8])
        c_bn = sb("c_bn", [4, 6])
        c_mv = sb("c_mv", [4, 2])
        c_rs = sb("c_rs", [4, 2])
        l_bn = sb("l_bn", [NT, 6])
        l_mv = sb("l_mv", [NT, 2])
        l_rs = sb("l_rs", [4, NT])
        f_stats = rows[:, 0, :]
        affine = sb("affine", [4, KT])
        gates2 = sb("gates2", [4])
        b1t = sb("b1t", [E * MT])
        gb = sb("gb", [E * MT])
        wrt = sb("wrt", [KT, E])
        brb = sb("brb", [E])
        affine_raw = l_aff[0:4 * KT, 0, 0:P]
        tgate = gates2[:, 2:3]
        fgate = gates2[:, 3:4]
        f_logit = rot_c[:, 0:64].rearrange("p (t e) -> p t e", e=E)
        f_tmp = rot_c[:, 64:128].rearrange("p (t e) -> p t e", e=E)
        f_rank = rot_c[:, 128:192].rearrange("p (t e) -> p t e", e=E)
        f_gate = rot_c[:, 192:256].rearrange("p (t e) -> p t e", e=E)
        f_max = rot_s[:, 0:16]
        f_sum = rot_s[:, 16:32]
        f_inv = rot_s[:, 32:48]
        f_bn = f_stats[:, 0:96].rearrange("p (t c) -> p t c", c=6)
        f_mv = f_stats[:, 96:128].rearrange("p (t c) -> p t c", c=2)
        f_rs = f_stats[:, 128:160].rearrange("p (a t) -> p a t", a=2)
        bo_b = c_aff[:].rearrange("p k n -> p (k n)")
        csum = recip[:, 0:D]
        f_rows = lat_r[:]
        b2b = acc[:, 0, :].rearrange("p (e d) -> p e d", e=E)
        xt_raw = l_aff[:]
        hid = pall[:, 0:4 * N].rearrange("p (r n) -> p r n", r=4)

        sc = [ps("sc0", 2 * N), ps("sc1", 2 * N)]
        pv = ps("pv", N)
        kv = ps("kv", 2 * UW)
        tr = ps("tr", N)
        mi = ps("mi", N)
        hb = [sc[0][:, 0:N], sc[0][:, N:2 * N], kv[:], pv[:]]
        yb = [[sc[1][:, 0:N], sc[1][:, N:2 * N]], [tr[:], mi[:]]]

        ld_ctx = [sem(f"ld_ctx{i}") for i in range(4)]
        ld_x = [sem("ld_x0"), sem("ld_x1")]
        ld_w = [sem(f"ld_w{i}") for i in range(4)]
        ld_aff = sem("ld_aff")
        aff_turned = sem("aff_turned")
        aff_ready = sem("aff_ready")
        ld_rope = sem("ld_rope")
        ld_small = sem("ld_small")
        ld_wq = sem("ld_wq")
        ld_wo = sem("ld_wo")
        const = sem("const")
        wkv_h = sem("wkv_h")
        wkv_ready = sem("wkv_ready")
        tanh_ready = sem("tanh_ready")
        c_st = sem("c_st")
        c_ag = sem("c_ag")
        c_e1 = sem("c_e1")
        c_rstd = sem("c_rstd")
        c_norm = sem("c_norm")
        c_tr = sem("c_tr")
        c_affd = sem("c_affd")
        c_high = sem("c_high")
        c_ready = sem("c_ready")
        l_st = sem("l_st")
        l_ag = sem("l_ag")
        l_ch = sem("l_ch")
        l_scale = sem("l_scale")
        l_norm = sem("l_norm")
        l_tr = sem("l_tr")
        l_affd = sem("l_affd")
        l_ready = sem("l_ready")
        wq_high = sem("wq_high")
        wq_ready = sem("wq_ready")
        wo_high = sem("wo_high")
        wo_ready = sem("wo_ready")
        kv_ready = sem("kv_ready")
        kraw_out = sem("kraw_out")
        kv_out = sem("kv_out")
        rot1 = sem("rot1")
        rot2 = sem("rot2")
        rot = sem("rot")
        k_tr = sem("k_tr")
        k_out = sem("k_out")
        k_ready = sem("k_ready")
        kst_ready = [sem("kst_ready0"), sem("kst_ready1")]
        q_mm = sem("q_mm")
        q_high = sem("q_high")
        q_ready = sem("q_ready")
        q_doubled = sem("q_doubled")
        sc_ready = [sem("sc_ready0"), sem("sc_ready1")]
        exp_done = [sem("exp_done0"), sem("exp_done1")]
        clamped = [sem("clamped0"), sem("clamped1")]
        summed = [sem("summed0"), sem("summed1")]
        pv_done = sem("pv_done")
        den_ready = sem("den_ready")
        rec_done = sem("rec_done")
        o_norm = sem("o_norm")
        o_high = sem("o_high")
        o_ready = sem("o_ready")
        wo_mm = sem("wo_mm")
        wo_out = sem("wo_out")
        ld_bo = sem("ld_bo")
        ld_b2 = sem("ld_b2")
        f_ldw = [sem("f_ldw0"), sem("f_ldw1")]
        f_bo = sem("f_bo")
        f_stat = sem("f_stat")
        f_agg = sem("f_agg")
        f_eps = sem("f_eps")
        f_rstd = sem("f_rstd")
        f_norm = sem("f_norm")
        f_tr = sem("f_tr")
        f_raw = sem("f_raw")
        f_xready = sem("f_xready")
        f_lmm = sem("f_lmm")
        f_lout = sem("f_lout")
        f_chain = sem("f_chain")
        f_diff = sem("f_diff")
        f_exp = sem("f_exp")
        gb_done = sem("gb_done")
        gbh = sem("gbh")
        gb_ready = sem("gb_ready")
        w_high = [sem("w_high0"), sem("w_high1")]
        w_ready = [sem("w_ready0"), sem("w_ready1")]
        ld_p = [sem("ld_p0"), sem("ld_p1")]
        p_high = sem("p_high")
        p_ready = sem("p_ready")
        h_mm = sem("h_mm")
        h_act = sem("h_act")
        h_high = sem("h_high")
        h_ready = sem("h_ready")
        y_mm = sem("y_mm")
        y_out = sem("y_out")
        cs_mm = sem("cs_mm")
        cs_chain = sem("cs_chain")
        fin = sem("fin")
        stored = sem("stored")

        def step_no(b, u, s):
            return b * BS + (u * STEPS + s)

        def tile_no(b, t):
            return b * ST + t

        def kv_no(b, u, t):
            return b * BS + (u * ST + t)

        def pair_no(b, p):
            return b * PAIRS + p

        QH = N // 2

        TURN = BS - ST - 6
        NORM, SCALE, LOAD = TURN - 1, TURN - 2, TURN - 4
        L_TURN = TURN + ST
        L_AGG, L_NORM = SCALE - NT - 1, SCALE

        def wait(eng, semaphore, count):
            if not (isinstance(count, int) and count <= 0):
                eng.wait_ge(semaphore, count)

        ROWS = STEPS + 1
        HALVES = 2 * B
        EARLY = (B - 1) * NT

        PIECE = 2
        PIECES = 4

        def piece_raw(piece):
            return wraw[:, (piece % 2) * 1024:(piece % 2 + 1) * 1024]

        def piece_of(piece, part):
            at = (piece // 2) * 4096 + part * 2048 + (piece % 2) * 1024
            return big[0][:, at:at + 1024]

        def half_at(u, s, last):
            return s if last and u == UNITS - 1 and s < HALVES - 2 else None

        def attention(eng, before, step):
            before()
            for s in range(STEPS):
                step(0, 0, s, False)
            with eng.Fori(0, B - 1) as b:
                for u in range(1, UNITS + 1):
                    for s in range(STEPS):
                        step(b + u // UNITS, u % UNITS, s, False)
            for u in range(1, UNITS):
                for s in range(STEPS):
                    step(B - 1, u, s, True)

        SLOTS = ST + 3

        def is_first(b, u):
            return isinstance(b, int) and b == 0 and u == 0

        def next_unit(b, u):
            return (b, u + 1) if u + 1 < UNITS else (b + 1, 0)

        def next_pair(b, p):
            return (b, p + 1) if p + 1 < PAIRS else (b + 1, 0)

        block = stack.enter_context(nc.Block())

        @block.sync
        def _(sp):
            def bcast(v):
                return v.rearrange("(a n) -> a n", a=1).to_broadcast([P, v.shape[0]])

            def load_ctx(b, t):
                wait(sp, c_tr, tile_no(b, t) - 3)
                src = ctx_in[b] if isinstance(b, int) else ctx_in[bass.ds(b, 1)].rearrange("a s d -> (a s) d")
                sp.dma_start(rows[:, t % 4, :], src[t * P:(t + 1) * P, :]).then_inc(ld_ctx[t % 4], 16)

            def load_wq(b, u):
                if isinstance(b, int) and b * UNITS + u == 1:
                    sp.wait_ge(wq_ready, 1)
                wait(sp, wo_ready, b * UNITS + u - 1)
                sp.dma_start(w_raw[:], w_q[:, u * UW:(u + 1) * UW].rearrange("(k p) n -> p k n", p=P)).then_inc(ld_wq, 16)

            def load_wo(b, u, last):
                if last and u == UNITS - 1:
                    sp.wait_ge(wo_ready, b * UNITS + u)
                else:
                    sp.wait_ge(wq_ready, b * UNITS + u + 2)
                sp.dma_start(w_raw[:], w_o[u * UW:(u + 1) * UW, :].rearrange("(q p) n -> p q n", p=P)).then_inc(ld_wo, 16)

            def q_double(b, p):
                sp.wait_ge(q_ready, pair_no(b, p) + 1)
                for h in range(2):
                    for half in range(2):
                        sp.dma_start(q_sp[half * DH:(half + 1) * DH, p % 2, h, :, :].bitcast(F32),
                                     q_pair[h * DH:(h + 1) * DH, :, :].bitcast(F32)).then_inc(q_doubled, 16)

            def k_store(b, u, t):
                sp.wait_ge(k_ready, kv_no(b, u, t) + 1)
                for l in range(2):
                    for h in range(2):
                        dst = kst[l * DH:(l + 1) * DH, u % 2, :, t * P:(t + 1) * P].rearrange("p (j h) s -> p j h s", h=2)
                        sp.dma_start(dst[:, :, h, :].bitcast(F32),
                                     k_t[h * DH:(h + 1) * DH, t % 2, l, :].rearrange("p (j s) -> p j s", j=2).bitcast(F32)
                                     ).then_inc(kst_ready[t % 2], 16)

            def load_wkv(u):
                for k in range(KT):
                    sp.dma_start(wkv_raw[:, u, k], w_kv[k * P:(k + 1) * P, :].rearrange("p (w n) -> p w n", w=2)
                                 [:, :, u * UW:(u + 1) * UW]).then_inc(ld_w[u], 16)

            def before():
                load_ctx(0, 0)
                load_ctx(0, 1)
                load_wkv(0)
                load_ctx(0, 2)
                sp.dma_start(cosb[:], cos.rearrange("(t p) c -> p t c", p=P)).then_inc(ld_rope, 16)
                sp.dma_start(sinb[:, :, 1, :], sin.rearrange("(t p) c -> p t c", p=P)).then_inc(ld_rope, 16)
                load_ctx(0, 3)
                sp.dma_start(xacc[:, 0:NT, :], x[0].rearrange("(a p) d -> p a d", p=P)).then_inc(ld_x[0], 16)
                load_wq(0, 0)
                for u in range(1, UNITS):
                    load_wkv(u)
                    load_ctx(0, 3 + u)
                for t in range(3 + UNITS, ST):
                    load_ctx(0, t)
                for t in range(ST - 1):
                    if t == 4:
                        q_double(0, 0)
                    k_store(0, 0, t)
                sp.dma_start(gates2[:, 0:1], bcast(g_xattn)).then_inc(ld_small, 16)
                sp.dma_start(gates2[:, 1:2], bcast(g_ffn)).then_inc(ld_small, 16)
                sp.dma_start(brb[:], bcast(b_r)).then_inc(ld_small, 16)
                with nc.allow_non_contiguous_dma(reason="small vectors of the experts"):
                    sp.dma_start(b1t[:], b_1.rearrange("e (m p) -> p (e m)", p=P)).then_inc(ld_small, 16)
                    sp.dma_start(wrt[:], w_r.rearrange("(k p) e -> p k e", p=P)).then_inc(ld_small, 16)
                for t in range(1, B):
                    sp.dma_start(xacc[:, t * NT:(t + 1) * NT, :], x[t].rearrange("(a p) d -> p a d", p=P)).then_inc(ld_x[1], 16)

            def step(b, u, s, last):
                if s == 0:
                    nb, nu = next_unit(b, u)
                    if not (last and u == UNITS - 1):
                        load_wq(nb, nu)
                if s == 4:
                    load_wo(b, u, last)
                i, p = u * STEPS + s, u * 2 + s // CH
                if s % CH == 2 and not (last and p == PAIRS - 1):
                    q_double(*next_pair(b, p))
                if s == 0:
                    k_store(b, u, ST - 1)
                elif not (last and u == UNITS - 1):
                    k_store(*next_unit(b, u), s - 1)
                if not last and 0 <= i - LOAD < ST:
                    load_ctx(b + 1, i - LOAD)
                if last and i == STEPS:
                    sp.wait_ge(c_ready, B * ST)
                    sp.dma_start(bo_b, bcast(b_o)).then_inc(ld_bo, 16)
                if last and u == UNITS - 1:
                    for piece, at in enumerate((1, 1, 4, 5)):
                        if s == at:
                            load_piece(piece)

            def load_piece(piece):
                sp.wait_ge(pv_done, (B - 1) * BS + BS - STEPS)
                wait(sp, p_ready, piece - 1)
                sp.dma_start(piece_raw(piece).rearrange("p (k n) -> p k n", k=(1, 4)[piece // 2]),
                             (w_1[0], w_2[0])[piece // 2].rearrange("(a k p) n -> a p k n", a=2, p=P)[piece % 2]
                             ).then_inc(ld_p[piece % 2], 16)

            def load_expert(e, half):
                view = (w_1[e].rearrange("(k p) n -> p k n", p=P), w_2[e].rearrange("(m p) n -> p m n", p=P))[half]
                sp.dma_start(wraw[:, half * 2048:(half + 1) * 2048].rearrange("p (k n) -> p k n", k=view.shape[1]),
                             view).then_inc(f_ldw[half], 16)

            attention(sp, before, step)
            sp.wait_ge(p_ready, PIECES)
            load_expert(1, 0)
            sp.wait_ge(pv_done, B * BS)
            load_expert(1, 1)
            sp.wait_ge(rec_done, B * PAIRS)
            sp.dma_start(b2b, b_2.rearrange("(a e) n -> a e n", a=1).to_broadcast([P, E, D])).then_inc(ld_b2, 16)
            for e in range(2, E):
                for half in range(2):
                    sp.wait_ge(w_ready[half], e - 1)
                    load_expert(e, half)
            for t in range(NT):
                sp.wait_ge(fin, t + 1)
                sp.dma_start(out[t].rearrange("(a p) d -> p a d", p=P), xacc[:, t * NT:(t + 1) * NT, :]).then_inc(stored, 16)
            sp.wait_ge(stored, 16 * NT)

        @block.gpsimd
        def _(pool):
            g = nc.gpsimd

            def ctx_scale(b, t):
                pool.wait_ge(c_ag, tile_no(b, t) + 1)
                g.tensor_tensor(c_rs[:, t % 4, 0:1], c_mv[:, t % 4, 1:2], eps[:, 0:1], ALU.add).then_inc(c_e1, 1)
                pool.wait_ge(c_e1, tile_no(b, t) + 1)
                g.tensor_tensor(c_rs[:, t % 4, 1:2], c_rs[:, t % 4, 0:1], mhalf[:, 0:1], ALU.pow).then_inc(c_rstd, 1)

            def lat_scale(b):
                pool.wait_ge(l_ag, b * NT + NT)
                v = l_mv[:, :, 1]
                e1, r, w, e2 = (l_rs[:, i, :] for i in range(4))
                n = [b * 6]

                def chain(ins):
                    n[0] = n[0] + 1
                    ins.then_inc(l_ch, 1)
                    pool.wait_ge(l_ch, n[0])

                chain(g.tensor_tensor(e1, v, eps[:, 0:NT], ALU.add))
                chain(g.tensor_tensor(r, e1, mhalf[:, 0:NT], ALU.pow))
                chain(g.tensor_tensor(w, r, r, ALU.mult))
                chain(g.tensor_tensor(w, w, v, ALU.mult))
                chain(g.tensor_tensor(w, w, eps[:, 0:NT], ALU.add))
                chain(g.tensor_tensor(e2, w, mhalf[:, 0:NT], ALU.pow))
                g.tensor_tensor(e1, e2, r, ALU.mult).then_inc(l_scale, 1)

            def wq_low(b, u):
                pool.wait_ge(wq_high, b * UNITS + u + 1)
                g.tensor_tensor(wq[:, 1], w_raw[:], wq[:, 0].bitcast(F32), ALU.subtract).then_inc(wq_ready, 1)

            def wo_low(b, u):
                pool.wait_ge(wo_high, b * UNITS + u + 1)
                g.tensor_tensor(wo[:, 1], w_raw[:], wo[:, 0].bitcast(F32), ALU.subtract).then_inc(wo_ready, 1)

            def k_low(b, u, t):
                pool.wait_ge(k_out, kv_no(b, u, t) + 1)
                g.tensor_tensor(k_t[:, t % 2, 1, :], k_whole[:], k_t[:, t % 2, 0, :].bitcast(F32),
                                ALU.subtract).then_inc(k_ready, 1)

            def rotate(b, u, t):
                n = kv_no(b, u, t)
                kh = k_raw[:].rearrange("p (h a c) -> p h a c", h=4, a=2)
                pool.wait_ge(kraw_out, n + 1)
                g.tensor_tensor(rot_s[:].rearrange("p (h a c) -> p h a c", h=4, a=2), kh[:, :, ::-1, :],
                                sinb[:, t].unsqueeze(1).to_broadcast([P, 4, 2, HALF]), ALU.mult).then_inc(rot2, 1)
                pool.wait_ge(rot1, n + 1)
                pool.wait_ge(rot2, n + 1)
                g.tensor_tensor(k_rot[:], rot_c[:], rot_s[:], ALU.add).then_inc(rot, 1)

            def rows_scale(t):
                pool.wait_ge(f_agg, NT * (t + 1))
                sl = slice(NT * t, NT * (t + 1))
                g.tensor_tensor(f_rs[:, 0, sl], f_mv[:, sl, 1], eps[:, 0:NT], ALU.add).then_inc(f_eps, 1)
                pool.wait_ge(f_eps, t + 1)
                g.tensor_tensor(f_rs[:, 1, sl], f_rs[:, 0, sl], mhalf[:, 0:NT], ALU.pow).then_inc(f_rstd, 1)

            def x_low(hf):
                pool.wait_ge(f_raw, hf + 1)
                t, sl = hf // 2, slice((hf % 2) * QH, (hf % 2 + 1) * QH)
                g.tensor_tensor(x_t[:, t, 1, :, sl], xt_raw, x_t[:, t, 0, :, sl].bitcast(F32), ALU.subtract).then_inc(f_xready, 1)

            def piece_low(piece):
                pool.wait_ge(p_high, piece + 1)
                g.tensor_tensor(piece_of(piece, 1), piece_raw(piece), piece_of(piece, 0).bitcast(F32),
                                ALU.subtract).then_inc(p_ready, 1)

            def w_low(e, half):
                pool.wait_ge(w_high[half], e)
                w = big[e % 2][:, half * 4096:(half + 1) * 4096].rearrange("p (l n) -> p l n", l=2)
                g.tensor_tensor(w[:, 1, :], wraw[:, half * 2048:(half + 1) * 2048], w[:, 0, :].bitcast(F32),
                                ALU.subtract).then_inc(w_ready[half], 1)

            def before():
                g.memset(ident[:], 0.0).then_inc(const, 1)
                g.memset(mhalf[:], -0.5).then_inc(const, 1)
                g.memset(eps[:], EPS).then_inc(const, 1)
                g.memset(ones[:], 1.0).then_inc(const, 1)
                pool.wait_ge(const, 4)
                g.affine_select(out=ident[:], in_=ident[:], compare_op=ALU.not_equal, fill=1.0, base=0,
                                pattern=[[-1, P]], channel_multiplier=1).then_inc(const, 1)
                for t in range(SLOTS):
                    if t < ST:
                        ctx_scale(0, t)
                    if t == 3:
                        pool.wait_ge(const, 6)
                    if 0 <= t - 3 < ST:
                        rotate(0, 0, t - 3)
                    if t == 3:
                        lat_scale(0)
                    if t == 5:
                        wq_low(0, 0)

            def step(b, u, s, last):
                i = u * STEPS + s
                make = not (last and u == UNITS - 1)
                if make:
                    rotate(*next_unit(b, u), s)
                if s == 0:
                    k_low(b, u, ST - 1)
                elif make:
                    k_low(*next_unit(b, u), s - 1)
                    if s == 3:
                        wq_low(*next_unit(b, u))
                if s == 7:
                    wo_low(b, u)
                if not last and 0 <= i - SCALE < ST:
                    ctx_scale(b + 1, i - SCALE)
                if not last and i == L_NORM - 1:
                    lat_scale(b + 1)
                if last and i in (ROWS + NT + 1, ROWS + 2 * NT + 1, ROWS + 3 * NT + 1):
                    rows_scale((i - ROWS) // NT - 1)
                if half_at(u, s, last) is not None:
                    x_low(s)
                if last and u == UNITS - 1 and PIECE <= s < PIECE + PIECES:
                    piece_low(s - PIECE)

            attention(pool, before, step)

            rows_scale(B - 1)
            x_low(HALVES - 2)
            x_low(HALVES - 1)
            for e in range(1, E):
                for half in range(2):
                    w_low(e, half)

        @block.scalar
        def _(act):
            a = nc.scalar

            def bcast(v):
                return v.rearrange("(a n) -> a n", a=1).to_broadcast([P, v.shape[0]])

            def k_split(b, u, t):
                act.wait_ge(k_tr, kv_no(b, u, t) + 1)
                wait(act, k_ready, kv_no(b, u, t))
                if not (isinstance(b, int) and kv_no(b, u, t) < 2):
                    act.wait_ge(kst_ready[t % 2], kv_no(b, u, t) // 2 * 64 if isinstance(b, int)
                                else b * (BS // 2 * 64) + (u * ST + t) // 2 * 64)
                a.activation(k_t[:, t % 2, 0, :], tr[:, 0:UW], ACT.Copy)
                a.activation(k_whole[:], tr[:, 0:UW], ACT.Copy).then_inc(k_out, 1)

            def kv_evac(b, u, t):
                act.wait_ge(kv_ready, kv_no(b, u, t) + 1)
                wait(act, rot, kv_no(b, u, t))
                a.activation(k_raw[:], kv[:, 0:UW], ACT.Copy).then_inc(kraw_out, 1)
                a.activation(val[:, u % 2, t, :], kv[:, UW:2 * UW], ACT.Copy).then_inc(kv_out, 1)

            def ctx_affine(b, t, bank, high=True):
                act.wait_ge(c_tr, tile_no(b, t) + 1)
                wait(act, c_ready, tile_no(b, t))
                for dst in ((ctx_t[:, 0, :, t * P:(t + 1) * P], c_aff) if high else (c_aff,)):
                    for k in range(KT):
                        last = a.activation(dst[:, k, :], bank[:, k * P:(k + 1) * P], ACT.Identity,
                                            scale=affine[:, 2, k:k + 1], bias=affine[:, 3, k:k + 1])
                last.then_inc(c_affd, 1)

            def lat_affine(b, hf, bank):
                act.wait_ge(l_tr, b * 2 + hf + 1)
                wait(act, l_ready, b * 2 + hf)
                for dst in (lat_t[:, 0, :, hf * QH:(hf + 1) * QH], l_aff):
                    for k in range(KT):
                        last = a.activation(dst[:, k, :], bank[:, k * QH:(k + 1) * QH], ACT.Identity,
                                            scale=affine[:, 0, k:k + 1], bias=affine[:, 1, k:k + 1])
                last.then_inc(l_affd, 1)

            def o_round(b, p):
                act.wait_ge(o_norm, pair_no(b, p) + 1)
                a.activation(o_sp[:, 0, p % 2, :], recip[:], ACT.Copy).then_inc(o_high, 1)

            def wkv_round(u):
                act.wait_ge(ld_w[u], 16 * KT)
                for w in range(2):
                    last = a.activation(wkv[:, 0, :, w * INNER + u * UW:w * INNER + (u + 1) * UW], wkv_raw[:, u, :, w, :],
                                        ACT.Copy)
                last.then_inc(wkv_h, 1)

            def wq_round(b, u):
                act.wait_ge(ld_wq, (b * UNITS + u + 1) * 16)
                a.activation(wq[:, 0], w_raw[:], ACT.Copy).then_inc(wq_high, 1)

            def wo_round(b, u):
                act.wait_ge(ld_wo, (b * UNITS + u + 1) * 16)
                a.activation(wo[:, 0], w_raw[:], ACT.Copy).then_inc(wo_high, 1)

            def q_round(b, p):
                act.wait_ge(q_mm, pair_no(b, p) + 1)
                wait(act, q_doubled, pair_no(b, p) * 64)
                a.activation(q_pair[:, 0, :], mi[:], ACT.Copy).then_inc(q_high, 1)

            def exps(b, u, s, h):
                act.wait_ge(sc_ready[h], step_no(b, u, s) + 1)
                c, q = s % CH, pair_no(b, u * 2 + s // CH)
                wait(act, summed[h], q * 4 + (-2, -1, 1, 1)[c])
                a.activation(prob[:, s % 2, h, :], sc[h][:], ACT.Exp, scale=DH ** -0.5).then_inc(exp_done[h], 1)

            def x_out(hf):
                act.wait_ge(f_tr, hf + 1)
                wait(act, f_xready, hf)
                wait(act, f_lmm, hf)
                t, sl = hf // 2, slice((hf % 2) * QH, (hf % 2 + 1) * QH)
                src = tr[:].rearrange("p (k n) -> p k n", k=KT)
                a.activation(x_t[:, t, 0, :, sl], src, ACT.Copy)
                a.activation(xt_raw, src, ACT.Copy).then_inc(f_raw, 1)

            def piece_round(piece):
                act.wait_ge(ld_p[piece % 2], 16 * (piece // 2 + 1))
                a.activation(piece_of(piece, 0), piece_raw(piece), ACT.Copy).then_inc(p_high, 1)

            def before():
                for i, v in enumerate((lat_g, lat_b, ctx_g, ctx_b)):
                    act.dma_start(affine_raw[i * KT:(i + 1) * KT, :], v.rearrange("(k p) -> k p", p=P)).then_inc(ld_aff, 16)
                wkv_round(0)
                act.wait_ge(aff_turned, 1)
                a.activation(affine[:].rearrange("p v k -> p (v k)"), mi[:, 0:4 * KT], ACT.Copy).then_inc(aff_ready, 1)
                act.wait_ge(aff_ready, 1)
                for t in range(SLOTS):
                    if 0 <= t - 3 < ST:
                        kv_evac(0, 0, t - 3)
                    if 0 <= t - 4 < ST - 1:
                        k_split(0, 0, t - 4)
                    if 0 <= t - 1 < ST:
                        ctx_affine(0, t - 1, sc[0][:, ((t - 1) % 2) * N:((t - 1) % 2 + 1) * N], high=False)
                    if t == 4:
                        wq_round(0, 0)
                    if t in (5, 6):
                        lat_affine(0, t - 5, sc[1][:, (t - 5) * N:(t - 4) * N])
                    if t == 7:
                        q_round(0, 0)
                    if t in (3, 5, 7):
                        wkv_round(t // 2)

            def step(b, u, s, last):
                i = u * STEPS + s
                p, c = u * 2 + s // CH, s % CH
                make = not (last and u == UNITS - 1)
                exps(b, u, s, 0)
                exps(b, u, s, 1)
                if make:
                    kv_evac(*next_unit(b, u), s)
                if s == 0:
                    k_split(b, u, ST - 1)
                elif make:
                    k_split(*next_unit(b, u), s - 1)
                if c == 1 and not (is_first(b, u) and s == 1):
                    o_round(*((b, p - 1) if p else (b - 1, PAIRS - 1)))
                if s == 3 and make:
                    wq_round(*next_unit(b, u))
                if s == 7:
                    wo_round(b, u)
                if is_first(b, u) and s == 4:
                    act.wait_ge(ld_small, 16 * 5)
                    a.activation(gates2[:, 2:4], gates2[:, 0:2], ACT.Tanh).then_inc(tanh_ready, 1)
                if not last and 0 <= i - TURN < ST:
                    ctx_affine(b + 1, i - TURN, tr)
                if not last and 0 <= i - L_TURN < 2:
                    lat_affine(b + 1, i - L_TURN, tr)
                if c == 1 and not (last and p == PAIRS - 1):
                    q_round(*next_pair(b, p))

                if half_at(u, s, last) is not None:
                    x_out(s)
                if last and u == UNITS - 1 and PIECE <= s < PIECE + PIECES:
                    piece_round(s - PIECE)

            attention(act, before, step)

            def gelu(n, e, m):
                act.wait_ge(h_mm, n + 1)
                if not (isinstance(n, int) and n < 4):
                    act.wait_ge(h_ready, n - 3)
                a.activation(hid[:, m % 4, :], hb[m % 4], ACT.Gelu, bias=b1t[:, e * MT + m:e * MT + m + 1]).then_inc(h_act, 1)

            a.activation(gb[:], b1t[:], ACT.Gelu).then_inc(gb_done, 1)
            for n in range(B * MT):
                gelu(n, 0, n % MT)
                if n == 1:
                    o_round(B - 1, PAIRS - 1)
                if n == 6:
                    x_out(HALVES - 2)
                if n == 7:
                    x_out(HALVES - 1)
                if n == MT + 4:
                    act.wait_ge(f_diff, 1)
                    a.activation(f_tmp, f_logit, ACT.Exp).then_inc(f_exp, 1)
            for e in range(1, E):
                with act.Fori(0, B) as t:
                    for m in range(MT):
                        gelu(t * MT + (e * B * MT + m), e, m)

        @block.vector
        def _(dve):
            v = nc.vector

            def ctx_stats(b, t):
                dve.wait_ge(ld_ctx[t % 4], b * (16 * ST // 4) + 16 * (t // 4 + 1))
                v.bn_stats(c_bn[:, t % 4, :], rows[:, t % 4, :]).then_inc(c_st, 1)

            def ctx_aggregate(b, t):
                v.bn_aggr(c_mv[:, t % 4, :], c_bn[:, t % 4, :]).then_inc(c_ag, 1)

            def ctx_norm(b, t):
                dve.wait_ge(c_rstd, tile_no(b, t) + 1)
                v.tensor_scalar(rows[:, t % 4, :], rows[:, t % 4, :], c_mv[:, t % 4, 0:1], c_rs[:, t % 4, 1:2],
                                ALU.subtract, ALU.mult).then_inc(c_norm, 1)

            def ctx_low(b, t):
                dve.wait_ge(c_affd, tile_no(b, t) + 1)
                v.tensor_tensor(ctx_t[:, 1, :, t * P:(t + 1) * P], c_aff[:], ctx_t[:, 0, :, t * P:(t + 1) * P].bitcast(F32),
                                ALU.subtract).then_inc(c_ready, 1)

            def ctx_split(t):
                dve.wait_ge(c_affd, t + 1)
                v.tensor_copy(ctx_t[:, 0, :, t * P:(t + 1) * P], c_aff[:]).then_inc(c_high, 1)
                dve.wait_ge(c_high, t + 1)
                v.tensor_tensor(ctx_t[:, 1, :, t * P:(t + 1) * P], c_aff[:], ctx_t[:, 0, :, t * P:(t + 1) * P].bitcast(F32),
                                ALU.subtract).then_inc(c_ready, 1)

            def k_low(t):
                dve.wait_ge(k_out, t + 1)
                v.tensor_tensor(k_t[:, t % 2, 1, :], k_whole[:], k_t[:, t % 2, 0, :].bitcast(F32),
                                ALU.subtract).then_inc(k_ready, 1)

            def lat_stats(b, t):
                first = isinstance(b, int) and b == 0
                dve.wait_ge(ld_x[0 if first else 1], 16 if first else 16 * (B - 1))
                row = xacc[:, t, :] if isinstance(b, int) else xacc[:, bass.ds(b * NT + t, 1), :].rearrange("p a d -> p (a d)")
                v.bn_stats(l_bn[:, t, :], row).then_inc(l_st, 1)

            def lat_aggregate(b, t):
                v.bn_aggr(l_mv[:, t, :], l_bn[:, t, :]).then_inc(l_ag, 1)

            def lat_norm(b, t):
                dve.wait_ge(l_scale, b + 1)
                row = xacc[:, t, :] if isinstance(b, int) else xacc[:, bass.ds(b * NT + t, 1), :].rearrange("p a d -> p (a d)")
                v.tensor_scalar(lat_r[:, t, :], row, l_mv[:, t, 0:1], l_rs[:, 0, t:t + 1],
                                ALU.subtract, ALU.mult).then_inc(l_norm, 1)

            def lat_low(b, hf):
                dve.wait_ge(l_affd, b * 2 + hf + 1)
                sl = slice(hf * QH, (hf + 1) * QH)
                v.tensor_tensor(lat_t[:, 1, :, sl], l_aff[:], lat_t[:, 0, :, sl].bitcast(F32),
                                ALU.subtract).then_inc(l_ready, 1)

            def wkv_low(u):
                dve.wait_ge(wkv_h, u + 1)
                for w in range(2):
                    cols = slice(w * INNER + u * UW, w * INNER + (u + 1) * UW)
                    last = v.tensor_tensor(wkv[:, 1, :, cols], wkv_raw[:, u, :, w, :], wkv[:, 0, :, cols].bitcast(F32),
                                           ALU.subtract)
                last.then_inc(wkv_ready, 1)

            def rot_cos(b, u, t):
                wait(dve, k_tr, kv_no(b, u, t))
                dve.wait_ge(kraw_out, kv_no(b, u, t) + 1)
                v.tensor_tensor(rot_c[:].rearrange("p (h c) -> p h c", h=8), k_raw[:].rearrange("p (h c) -> p h c", h=8),
                                cosb[:, t].unsqueeze(1).to_broadcast([P, 8, HALF]),
                                ALU.mult).then_inc(rot1, 1)

            def q_low(b, p):
                dve.wait_ge(q_high, pair_no(b, p) + 1)
                v.tensor_tensor(q_pair[:, 1, :], mi[:], q_pair[:, 0, :].bitcast(F32), ALU.subtract).then_inc(q_ready, 1)

            def clamp(b, u, s, h):
                dve.wait_ge(exp_done[h], step_no(b, u, s) + 1)
                v.tensor_scalar(prob[:, s % 2, h, :], prob[:, s % 2, h, :], EXP_LOW, EXP_HIGH,
                                ALU.max, ALU.min).then_inc(clamped[h], 1)

            def sums(b, u, s, h):
                c, q = s % CH, pair_no(b, u * 2 + s // CH)
                if c == 0:
                    return
                dve.wait_ge(clamped[h], step_no(b, u, s) + 1)
                if c == 1:
                    wait(dve, den_ready, q)
                    v.tensor_tensor(acc[:, h, :], prob[:, 0, h, :], prob[:, 1, h, :], ALU.add).then_inc(summed[h], 1)
                else:
                    dve.wait_ge(summed[h], q * 4 + c - 1)
                    v.tensor_tensor(acc[:, h, :], acc[:, h, :], prob[:, s % 2, h, :], ALU.add).then_inc(summed[h], 1)

            def fold(b, p, h):
                dve.wait_ge(summed[h], pair_no(b, p) * 4 + 3)
                v.tensor_tensor(acc[:, h, 0:N], acc[:, h, 0:N], acc[:, h, N:2 * N], ALU.add).then_inc(summed[h], 1)

            def reciprocals(b, p):
                dve.wait_ge(den_ready, pair_no(b, p) + 1)
                v.reciprocal(recip[:], mi[:]).then_inc(rec_done, 1)

            def normalise(b, p):
                dve.wait_ge(pv_done, (pair_no(b, p) + 1) * CH)
                dve.wait_ge(rec_done, pair_no(b, p) + 1)
                v.tensor_tensor(recip[:], pv[:], recip[:], ALU.mult).then_inc(o_norm, 1)

            def o_low(b, p):
                dve.wait_ge(o_high, pair_no(b, p) + 1)
                v.tensor_tensor(o_sp[:, 1, p % 2, :], recip[:], o_sp[:, 0, p % 2, :].bitcast(F32),
                                ALU.subtract).then_inc(o_ready, 1)

            def residual(b, u, hf):
                dve.wait_ge(wo_mm, (b * UNITS + u) * 2 + hf + 1)
                if isinstance(b, int):
                    dst = xacc[:, b * NT + 2 * hf:b * NT + 2 * hf + 2, :]
                else:
                    dst = xacc[:, bass.ds(b * NT + 2 * hf, 2), :]
                v.scalar_tensor_tensor(dst, mi[:].rearrange("p (a d) -> p a d", a=2), tgate, dst,
                                       ALU.mult, ALU.add).then_inc(wo_out, 1)

            def before():
                for t in range(SLOTS):
                    if t < ST:
                        ctx_stats(0, t)
                        dve.wait_ge(c_st, t + 1)
                        ctx_aggregate(0, t)
                    if 0 <= t - 1 < ST:
                        ctx_norm(0, t - 1)
                    if t == 2:
                        wkv_low(0)
                    if 0 <= t - 2 < ST:
                        ctx_split(t - 2)
                    if t == 2:
                        dve.wait_ge(ld_rope, 16 * 2)
                        v.tensor_scalar(sinb[:, :, 0, :], sinb[:, :, 1, :], -1.0, None, ALU.mult).then_inc(const, 1)
                        dve.wait_ge(const, 6)
                        for i in range(NT):
                            lat_stats(0, i)
                            dve.wait_ge(l_st, i + 1)
                            lat_aggregate(0, i)
                    if 0 <= t - 3 < ST:
                        rot_cos(0, 0, t - 3)
                    if 0 <= t - 4 < ST - 1:
                        k_low(t - 4)
                    if t == 4:
                        for i in range(NT):
                            lat_norm(0, i)
                    if t in (6, 7):
                        lat_low(0, t - 6)
                    if t == 8:
                        q_low(0, 0)
                    if t in (4, 6, 8):
                        wkv_low((t - 2) // 2)

            def step(b, u, s, last):
                i = u * STEPS + s
                p = u * 2 + s // CH
                c = s % CH
                make = not (last and u == UNITS - 1)
                last_pair = (b, p - 1) if p else (b - 1, PAIRS - 1)
                has_last = not (is_first(b, u) and s < CH)
                if c == 2 and not (last and p == PAIRS - 1):
                    q_low(*next_pair(b, p))
                if c == 1 and has_last:
                    normalise(*last_pair)
                if is_first(b, u) and s == STEPS - 1:
                    dve.wait_ge(tanh_ready, 1)
                ct, lt = i - SCALE, i - L_AGG
                if not last and 0 <= ct < ST:
                    dve.wait_ge(c_st, tile_no(b + 1, ct) + 1)
                if not last and 0 <= lt < NT:
                    dve.wait_ge(l_st, (b + 1) * NT + lt + 1)
                early = last and 0 <= i - ROWS - 1 < EARLY
                if early:
                    dve.wait_ge(f_stat, i - ROWS)
                clamp(b, u, s, 0)
                if early:
                    rows_aggregate(i - ROWS - 1)
                if not last and 0 <= ct < ST:
                    ctx_aggregate(b + 1, ct)
                if not last and 0 <= lt < NT:
                    lat_aggregate(b + 1, lt)
                clamp(b, u, s, 1)
                if make:
                    rot_cos(*next_unit(b, u), s)
                if not last and 0 <= i - TURN - 1 < ST:
                    ctx_low(b + 1, i - TURN - 1)
                if not last and 0 <= i - L_TURN - 1 < 2:
                    lat_low(b + 1, i - L_TURN - 1)
                sums(b, u, s, 0)
                if s in (2, 3) and not is_first(b, u):
                    residual(*((b, u - 1) if u else (b - 1, UNITS - 1)), s - 2)
                sums(b, u, s, 1)
                if c == CH - 1:
                    fold(b, p, 0)
                    fold(b, p, 1)
                if c == 0 and has_last:
                    reciprocals(*last_pair)
                if c == 1 and has_last:
                    o_low(*last_pair)
                if not last:
                    if 0 <= ct + 1 < ST:
                        ctx_stats(b + 1, ct + 1)
                    if 0 <= i - NORM < ST:
                        ctx_norm(b + 1, i - NORM)
                    if 0 <= lt + 1 < NT:
                        lat_stats(b + 1, lt + 1)
                    if 0 <= i - L_NORM < NT:
                        lat_norm(b + 1, i - L_NORM)

                if last and 0 <= i - ROWS < B * NT:
                    rows_bias(i - ROWS)
                if last and 0 <= i - ROWS < EARLY:
                    rows_stats(i - ROWS)
                if last and 0 <= i + 1 - (BS - STEPS) < HALVES - 2:
                    rows_norm(i + 1 - (BS - STEPS))
                if last and i == BS - 1:
                    logits(0, EARLY, kv)

            def rows_bias(j):
                dve.wait_ge(ld_bo, 16)
                v.scalar_tensor_tensor(xacc[:, j, :], bo_b, tgate, xacc[:, j, :], ALU.mult, ALU.add).then_inc(f_bo, 1)

            def rows_stats(j):
                dve.wait_ge(f_bo, j + 1)
                if j == EARLY:
                    dve.wait_ge(wo_out, B * UNITS * 2)
                v.bn_stats(f_bn[:, j, :], xacc[:, j, :]).then_inc(f_stat, 1)

            def rows_aggregate(j):
                v.bn_aggr(f_mv[:, j, :], f_bn[:, j, :]).then_inc(f_agg, 1)

            def rows_norm(hf):
                dve.wait_ge(f_rstd, hf // 2 + 1)
                wait(dve, f_tr, hf - 1)
                for i in range(2):
                    j = 2 * hf + i
                    v.tensor_scalar(f_rows[:, j % 4, :], xacc[:, j, :], f_mv[:, j, 0:1], f_rs[:, 1, j:j + 1],
                                    ALU.subtract, ALU.mult).then_inc(f_norm, 1)

            def logits(lo, hi, bank):
                if lo == 0:
                    dve.wait_ge(k_ready, B * BS)
                dve.wait_ge(f_lmm, hi // 2)
                v.tensor_tensor(f_logit[:, lo:hi, :], bank[:, 0:(hi - lo) * E].rearrange("p (t e) -> p t e", e=E),
                                brb[:].unsqueeze(1).to_broadcast([P, hi - lo, E]), ALU.add).then_inc(f_lout, 1)

            attention(dve, before, step)

            w1v = [big[i][:, 0:4096].rearrange("p (l n) -> p l n", l=2) for i in range(2)]
            w2v = [big[i][:, 4096:8192].rearrange("p (l n) -> p l n", l=2) for i in range(2)]

            def split_high(e, half):
                w = (w1v, w2v)[half][e % 2]
                dve.wait_ge(f_ldw[half], 16 * e)
                v.tensor_copy(w[:, 0, :], wraw[:, half * 2048:half * 2048 + 2048]).then_inc(w_high[half], 1)

            n_chain = [0]

            def chain(ins):
                n_chain[0] += 1
                ins.then_inc(f_chain, 1)
                dve.wait_ge(f_chain, n_chain[0])

            R = B * NT

            def gates_rank(j):
                if j == 0:
                    dve.wait_ge(f_lout, 2)
                    chain(v.tensor_reduce(f_max, f_logit, mybir.AxisListType.X, ALU.max))
                to = f_rank if j == 0 else f_gate
                for lo, hi, op in ((0, j + 1, ALU.is_gt), (j + 1, E, ALU.is_ge)):
                    if hi > lo:
                        chain(v.tensor_tensor(to[:, :, lo:hi], f_logit[:, :, j:j + 1].to_broadcast([P, R, hi - lo]),
                                              f_logit[:, :, lo:hi], op))
                if j:
                    chain(v.tensor_tensor(f_rank, f_rank, f_gate, ALU.add))
                if j == E - 1:
                    v.tensor_tensor(f_logit, f_logit, f_max.unsqueeze(2).to_broadcast([P, R, E]),
                                    ALU.subtract).then_inc(f_diff, 1)

            def gates_last():
                dve.wait_ge(f_exp, 1)
                chain(v.scalar_tensor_tensor(f_gate, f_rank, 2.0, f_tmp, ALU.is_lt, ALU.mult))
                chain(v.tensor_reduce(f_sum, f_gate, mybir.AxisListType.X, ALU.add))
                chain(v.reciprocal(f_inv, f_sum))
                chain(v.scalar_tensor_tensor(f_gate, f_gate, fgate, f_inv.unsqueeze(2).to_broadcast([P, R, E]),
                                             ALU.mult, ALU.mult))

            def b2_sum():
                dve.wait_ge(ld_b2, 16)
                chain(v.tensor_tensor(csum, b2b[:, 0, :], b2b[:, 1, :], ALU.add))
                for e in range(2, E):
                    chain(v.tensor_tensor(csum, csum, b2b[:, e, :], ALU.add))

            def gelu_b1():
                dve.wait_ge(gb_done, 1)
                v.tensor_copy(gb_sp[:, 0, :], gb[:]).then_inc(gbh, 1)
                dve.wait_ge(gbh, 1)
                v.tensor_tensor(gb_sp[:, 1, :], gb[:], gb_sp[:, 0, :].bitcast(F32), ALU.subtract).then_inc(gb_ready, 1)

            def biases(e):
                dve.wait_ge(cs_mm, e)
                chain(v.tensor_tensor(csum, hb[3][:, 0:D], csum, ALU.add))
                if e == E - 1:
                    chain(v.tensor_scalar(csum, csum, fgate, None, ALU.mult))

            def hidden(n, e, m):
                dve.wait_ge(h_act, n + 1)
                wait(dve, y_mm, n - 3)
                c = gb[:, e * MT + m:e * MT + m + 1]
                v.tensor_scalar(hid_sp[:, m % 4, 0, :], hid[:, m % 4, :], c, None, ALU.subtract).then_inc(h_high, 1)
                dve.wait_ge(h_high, n + 1)
                v.scalar_tensor_tensor(hid_sp[:, m % 4, 1, :], hid[:, m % 4, :], c, hid_sp[:, m % 4, 0, :].bitcast(F32),
                                       ALU.subtract, ALU.subtract).then_inc(h_ready, 1)

            def combine(e, t, parity):
                dve.wait_ge(y_mm, (t + e * B + 1) * MT)
                for i in range(NT):
                    if isinstance(t, int):
                        row, gate = xacc[:, t * NT + i, :], f_gate[:, t * NT + i, e:e + 1]
                    else:
                        row = xacc[:, bass.ds(t * NT + i, 1), :].rearrange("p a d -> p (a d)")
                        gate = f_gate[:, bass.ds(t * NT + i, 1), e:e + 1].rearrange("p a d -> p (a d)")
                    v.scalar_tensor_tensor(row, yb[parity][i // 2][:, (i % 2) * D:(i % 2 + 1) * D], gate, row,
                                           ALU.mult, ALU.add).then_inc(y_out, 1)
                if e == E - 1:
                    dve.wait_ge(y_out, (t + e * B + 1) * NT)
                    dst = xacc[:, bass.ds(t * NT, NT), :]
                    v.tensor_tensor(dst, dst, csum.unsqueeze(1).to_broadcast([P, NT, D]), ALU.add).then_inc(fin, 1)

            for n in range(B * MT):
                t, m = n // MT, n % MT
                hidden(n, 0, m)
                if t == 0:
                    if m == 0:
                        reciprocals(B - 1, PAIRS - 1)
                        normalise(B - 1, PAIRS - 1)
                    if m == 1:
                        o_low(B - 1, PAIRS - 1)
                    if m in (2, 3):
                        residual(B - 1, UNITS - 1, m - 2)
                    if m == 3:
                        for i in range(NT):
                            rows_stats(EARLY + i)
                        for i in range(NT):
                            dve.wait_ge(f_stat, EARLY + i + 1)
                            rows_aggregate(EARLY + i)
                    if m == 4:
                        rows_norm(HALVES - 2)
                    if m == 5:
                        rows_norm(HALVES - 1)
                    if m == 7:
                        logits(EARLY, B * NT, mi)
                if t == 1:
                    if m < E:
                        gates_rank(m)
                    if m == 5:
                        gates_last()
                    if m == 6:
                        combine(0, 0, 0)
                if t == 2:
                    if m == 0:
                        b2_sum()
                    if m == 1:
                        gelu_b1()
                    if m in (3, 5):
                        split_high(1, (m - 3) // 2)
                if t and m == MT - 1:
                    combine(0, t, t % 2)
            for e in range(1, E):
                biases(e)
                if e + 1 < E:
                    split_high(e + 1, 0)
                    split_high(e + 1, 1)
                with dve.Fori(0, B // 2) as d:
                    for r in range(2):
                        for m in range(MT):
                            hidden((d * 2 + r + e * B) * MT + m, e, m)
                        combine(e, d * 2 + r, r)

        @block.tensor
        def _(pe):
            mm = nc.tensor.matmul

            def three(dst, lhs, rhs, start, stop, **kw):
                mm(dst, lhs(0), rhs(0), start=start, stop=False, **kw)
                mm(dst, lhs(0), rhs(1), start=False, stop=False, **kw)
                return mm(dst, lhs(1), rhs(0), start=False, stop=stop, **kw)

            def ctx_turn(b, t, bank):
                pe.wait_ge(c_norm, tile_no(b, t) + 1)
                for k in range(KT):
                    last = nc.tensor.transpose(bank[:, k * P:(k + 1) * P], rows[:, t % 4, k * P:(k + 1) * P], ident[:])
                last.then_inc(c_tr, 1)

            def lat_turn(b, hf, bank):
                pe.wait_ge(l_norm, b * NT + 2 * hf + 2)
                for i in range(2):
                    for k in range(KT):
                        last = nc.tensor.transpose(bank[:, k * QH + i * P:k * QH + (i + 1) * P],
                                                   lat_r[:, 2 * hf + i, k * P:(k + 1) * P], ident[:])
                last.then_inc(l_tr, 1)

            def q_make(b, p):
                pe.wait_ge(l_ready, 2 * b + 2)
                pe.wait_ge(wq_ready, b * UNITS + p // 2 + 1)
                for k in range(KT):
                    last = three(mi[:], lambda l: wq[:, l, k, (p % 2) * P:(p % 2 + 1) * P],
                                 lambda l: lat_t[:, l, k, :], k == 0, k == KT - 1)
                last.then_inc(q_mm, 1)

            def kv_make(b, u, t):
                pe.wait_ge(c_ready, tile_no(b, t) + 1)
                wait(pe, kv_out, kv_no(b, u, t))
                for k in range(KT):
                    last = three(kv[:].rearrange("p (w n) -> p w n", w=2), lambda l: ctx_t[:, l, k, t * P:(t + 1) * P],
                                 lambda l: wkv[:, l, k, :].rearrange("p (w n) -> p w n", w=2)[:, :, u * UW:(u + 1) * UW],
                                 k == 0, k == KT - 1)
                last.then_inc(kv_ready, 1)

            def k_turn(b, u, t):
                pe.wait_ge(rot, kv_no(b, u, t) + 1)
                wait(pe, k_out, kv_no(b, u, t))
                for j in range(2):
                    last = nc.tensor.transpose(tr[:, j * P:(j + 1) * P], k_rot[:, j * P:(j + 1) * P], ident[:])
                last.then_inc(k_tr, 1)

            def score(b, u, s, h):
                c, j, p = s % CH, s // CH, u * 2 + s // CH
                if h == 0:
                    for i in range(2):
                        pe.wait_ge(kst_ready[i], b * (BS // 2 * 64) + (u * CH + c + 1) * 64)
                if c == 0 and h == 0:
                    pe.wait_ge(q_doubled, pair_no(b, p) * 64 + 64)
                wait(pe, exp_done[h], step_no(b, u, s))
                for i in range(2):
                    t = 2 * c + i
                    for l in range(2):
                        last = mm(sc[h][:, i * N:(i + 1) * N], kst[:, u % 2, 2 * j + h, t * P:(t + 1) * P],
                                  q_sp[:, j, h, l, :], start=l == 0, stop=l == 1)
                last.then_inc(sc_ready[h], 1)

            def values(b, u, s):
                c, j, p = s % CH, s // CH, u * 2 + s // CH
                if c == 0:
                    wait(pe, o_norm, pair_no(b, p))
                for h in range(2):
                    pe.wait_ge(clamped[h], step_no(b, u, s) + 1)
                for i in range(2):
                    for h in range(2):
                        last = mm(pv[h * DH:(h + 1) * DH, :], val[:, u % 2, 2 * c + i, (2 * j + h) * DH:(2 * j + h + 1) * DH],
                                  prob[:, s % 2, h, i * N:(i + 1) * N], start=c == 0 and i == 0, stop=c == CH - 1 and i == 1)
                last.then_inc(pv_done, 1)

            def denominators(b, p):
                for h in range(2):
                    pe.wait_ge(summed[h], (pair_no(b, p) + 1) * 4)
                    last = mm(mi[h * DH:(h + 1) * DH, :], ones[:], acc[:, h, 0:N], start=True, stop=True)
                last.then_inc(den_ready, 1)

            def project(b, u, hf):
                pe.wait_ge(o_ready, pair_no(b, 2 * u + 1) + 1)
                pe.wait_ge(wo_ready, b * UNITS + u + 1)
                for i in range(2):
                    for j in range(2):
                        last = three(mi[:, i * D:(i + 1) * D], lambda l: o_sp[:, l, j, (2 * hf + i) * P:(2 * hf + i + 1) * P],
                                     lambda l: wo[:, l, j, :], j == 0, j == 1)
                last.then_inc(wo_mm, 1)

            def x_turn(hf):
                pe.wait_ge(f_norm, 2 * hf + 2)
                for i in range(2):
                    for k in range(KT):
                        last = nc.tensor.transpose(tr[:, k * QH + i * P:k * QH + (i + 1) * P],
                                                   f_rows[:, (2 * hf + i) % 4, k * P:(k + 1) * P], ident[:])
                last.then_inc(f_tr, 1)

            def router(hf, bank, at):
                pe.wait_ge(f_raw, hf + 1)
                for i in range(2):
                    for k in range(KT):
                        last = mm(bank[:, (at + i) * E:(at + i + 1) * E], xt_raw[:, k, i * P:(i + 1) * P], wrt[:, k, :],
                                  start=k == 0, stop=k == KT - 1)
                last.then_inc(f_lmm, 1)

            def before():
                pe.wait_ge(const, 5)
                pe.wait_ge(ld_aff, 16 * 4)
                nc.tensor.transpose(mi[:, 0:4 * KT], affine_raw, ident[0:4 * KT, 0:4 * KT]).then_inc(aff_turned, 1)
                for t in range(SLOTS):
                    if 0 <= t - 3 < ST:
                        pe.wait_ge(wkv_ready, 1)
                        kv_make(0, 0, t - 3)
                    if 0 <= t - 4 < ST - 1:
                        k_turn(0, 0, t - 4)
                    if 0 <= t - 1 < ST:
                        wait(pe, c_affd, t - 2)
                        ctx_turn(0, t - 1, sc[0][:, ((t - 1) % 2) * N:((t - 1) % 2 + 1) * N])
                    if t in (5, 6):
                        lat_turn(0, t - 5, sc[1][:, (t - 5) * N:(t - 4) * N])
                    if t == 7:
                        q_make(0, 0)
                pe.wait_ge(wkv_ready, UNITS)

            def step(b, u, s, last):
                i = u * STEPS + s
                p, c = u * 2 + s // CH, s % CH
                make = not (last and u == UNITS - 1)
                nb, nu = next_unit(b, u)
                score(b, u, s, 0)
                score(b, u, s, 1)
                if half_at(u, s - 1, last) is not None and s:
                    router(s - 1, kv, 2 * (s - 1))
                if half_at(u, s, last) is not None and s:
                    x_turn(s)
                turned = not last and 0 <= i - TURN - 1 < ST + 2
                if make and turned:
                    kv_make(nb, nu, s)
                if s == 0 or make:
                    if turned and i - TURN - 1 < ST:
                        pe.wait_ge(c_affd, tile_no(b + 1, i - TURN - 1) + 1)
                    elif turned:
                        pe.wait_ge(l_affd, 2 * (b + 1) + i - L_TURN)
                    k_turn(*((nb, nu, s - 1) if s else (b, u, ST - 1)))
                if make and not turned:
                    kv_make(nb, nu, s)
                if c == 0 and not (is_first(b, u) and s == 0):
                    pe.wait_ge(q_ready, pair_no(b, p) + 1)
                    wait(pe, wo_out, (b * UNITS + u) * 2 - (2 if s == 0 else 0))
                    denominators(*((b, p - 1) if p else (b - 1, PAIRS - 1)))
                if s in (2, 3) and not is_first(b, u):
                    pe.wait_ge(q_ready, pair_no(b, p + 1) + 1)
                    wait(pe, wo_out, (b * UNITS + u) * 2 + s - 4)
                    project(*((b, u - 1) if u else (b - 1, UNITS - 1)), s - 2)
                if not (is_first(b, u) and s == 0):
                    values(*((b, u, s - 1) if s else (b, u - 1, STEPS - 1) if u else (b - 1, UNITS - 1, STEPS - 1)))
                if c == 1 and not (last and p == PAIRS - 1):
                    wait(pe, rec_done, pair_no(b, p))
                    q_make(*next_pair(b, p))
                if not last and TURN <= i < L_TURN + 2:
                    pe.wait_ge(k_out, kv_no(nb, nu, s - 1) + 1 if s else kv_no(b, u, ST - 1) + 1)
                    if i < L_TURN:
                        ctx_turn(b + 1, i - TURN, tr)
                    else:
                        lat_turn(b + 1, i - L_TURN, tr)
                if half_at(u, s, last) == 0:
                    pe.wait_ge(k_out, B * BS)
                    pe.wait_ge(kv_out, B * BS)
                    x_turn(0)

            attention(pe, before, step)
            values(B - 1, UNITS - 1, STEPS - 1)

            w1v = [big[i][:, 0:4096].rearrange("p (l k n) -> p l k n", l=2, k=KT) for i in range(2)]
            w2v = [big[i][:, 4096:8192].rearrange("p (l m n) -> p l m n", l=2, m=MT) for i in range(2)]

            def hidden(n, e, t, m):
                wait(pe, h_act, n - 3)
                if isinstance(t, int) and n == 3:
                    pe.wait_ge(o_norm, B * PAIRS)
                x_at = x_t[:, t] if isinstance(t, int) else x_t[:, bass.ds(t, 1)].rearrange("p a l k n -> p (a l) k n")
                for k in range(KT):
                    last = three(hb[m % 4], lambda l: w1v[e % 2][:, l, k, m * P:(m + 1) * P], lambda l: x_at[:, l, k, :],
                                 k == 0, k == KT - 1)
                last.then_inc(h_mm, 1)

            def outputs(n, e, t, m, parity):
                pe.wait_ge(h_ready, n + 1)
                if m == 0:
                    wait(pe, y_out, (t + e * B - 1) * NT)
                for i in range(NT):
                    last = three(yb[parity][i // 2][:, (i % 2) * D:(i % 2 + 1) * D],
                                 lambda l: hid_sp[:, m % 4, l, i * P:(i + 1) * P],
                                 lambda l: w2v[e % 2][:, l, m, :], m == 0 and i % 2 == 0, m == MT - 1 and i % 2 == 1,
                                 skip_group_check=True)
                last.then_inc(y_mm, 1)

            def block_of(e, t, parity, behind=lambda m: None):
                for m in range(3):
                    hidden((t + e * B) * MT + m, e, t, m)
                    behind(m - 3)
                for m in range(MT):
                    outputs((t + e * B) * MT + m, e, t, m, parity)
                    if m + 3 < MT:
                        hidden((t + e * B) * MT + m + 3, e, t, m + 3)
                    behind(m)

            def first_block(m):
                if m == -3:
                    denominators(B - 1, PAIRS - 1)
                    pe.wait_ge(f_lout, 1)
                    pe.wait_ge(p_ready, PIECES)
                if m == 1:
                    pe.wait_ge(rec_done, B * PAIRS)
                    project(B - 1, UNITS - 1, 0)
                if m == 2:
                    pe.wait_ge(wo_out, B * UNITS * 2 - 1)
                    project(B - 1, UNITS - 1, 1)
                if m == 4:
                    x_turn(HALVES - 2)
                if m == 5:
                    pe.wait_ge(wo_out, B * UNITS * 2)
                    router(HALVES - 2, mi, 0)
                    x_turn(HALVES - 1)
                if m == MT - 1:
                    router(HALVES - 1, mi, 2)

            def second_block(m):
                if m == -1:
                    pe.wait_ge(f_xready, HALVES)
                    pe.wait_ge(f_lout, 2)

            def biases(e, start):
                for m in range(MT):
                    last = three(hb[3][:, 0:D], lambda l: gb_sp[:, l, e * MT + m:e * MT + m + 1].to_broadcast([P, P]),
                                 lambda l: w2v[e % 2][:, l, m, :], start and m == 0, e > 0 and m == MT - 1)
                return last

            pe.wait_ge(f_xready, HALVES - 2)
            pe.wait_ge(p_ready, 2)
            block_of(0, 0, 0, first_block)
            for t in range(1, B):
                block_of(0, t, t % 2, second_block if t == 1 else lambda m: None)
            pe.wait_ge(gb_ready, 1)
            for e in range(1, E):
                pe.wait_ge(w_ready[0], e)
                pe.wait_ge(w_ready[1], e)
                pe.wait_ge(h_act, e * B * MT)
                if e == 1:
                    biases(0, True)
                biases(e, e > 1).then_inc(cs_mm, 1)
                with pe.Fori(0, B // 2) as d:
                    for r in range(2):
                        block_of(e, d * 2 + r, r)


INPUTS = ["x", "ctx_1024", "g_xattn", "g_ffn", "L0_xattn_cos", "L0_xattn_sin", "L0_xattn_ln_lat_g", "L0_xattn_ln_lat_b",
          "L0_xattn_ln_ctx_g", "L0_xattn_ln_ctx_b", "L0_xattn_Wq", "L0_xattn_Wkv", "L0_xattn_Wo", "L0_xattn_bo",
          "L0_ffn_w1", "L0_ffn_b1", "L0_ffn_w2", "L0_ffn_b2", "L0_ffn_wr", "L0_ffn_br"]


def kernel(**inputs):
    import numpy as np
    import concourse.bacc as bacc
    from concourse.bass_utils import run_bass_kernel_spmd

    nc = bacc.Bacc("TRN2", target_bir_lowering=False, num_devices=1)
    arrays, args = {}, []
    for name in INPUTS:
        value = np.ascontiguousarray(inputs[name])
        arrays[f"in_{name}"] = value
        args.append(nc.dram_tensor(f"in_{name}", value.shape, mybir.dt.from_np(value.dtype), kind="ExternalInput").ap())
    shape = inputs["x"].shape
    args.append(nc.dram_tensor("out", shape, F32, kind="ExternalOutput").ap())
    flamingo_kernel(nc, *args)
    return run_bass_kernel_spmd(nc, [arrays], core_ids=[0]).results[0]["out"]
```
